# Optimizing a Trainium2 kernel written in Bass

```python
import numpy as np
import jax
import jax.numpy as jnp

def _softmax(x, axis=-1):
    return jax.nn.softmax(x, axis=axis)

def _gelu(x):
    return jax.nn.gelu(x, approximate=True)

def _silu(x):
    return jax.nn.silu(x)

def _sigmoid(x):
    return jax.nn.sigmoid(x)

def _layernorm(x, axis=-1, eps=1e-05):
    m = jnp.mean(x, axis=axis, keepdims=True)
    v = jnp.var(x, axis=axis, keepdims=True)
    return (x - m) / jnp.sqrt(v + eps)

def _scatter_add(tgt, idx, src, axis=0):
    return tgt.at[idx].add(src)

def _segment_sum(src, seg, n):
    return jax.ops.segment_sum(src, seg, n)
kernel_name = 'mk_vit_tower_postln_d1_tok_img256_r4_772b8f'

def setup_inputs(seed: int=0):
    np.random.seed(seed)
    _w = jnp.asarray

    def _rec_inputs():
        import jax
        import jax.numpy as jnp
        _rk = jax.random.key(seed)
        x = -7.10856e-05 + 0.999911 * jax.random.normal(jax.random.fold_in(_rk, 1), (16, 64, 128, 64), jnp.float32)
        return x
    x = _rec_inputs()

    def _L0_tok_setup():
        import jax, jax.numpy as jnp
        import numpy as np
        PATCH_LEN = 16
        STRIDE = 8
        PAD = 8
        key = jax.random.key(seed)
        k1, k2 = jax.random.split(key)
        x = jax.random.normal(k1, (32, 64, 128, 64), dtype=jnp.float32)
        in_feat = 64 * (PATCH_LEN // 2 + 1) * 2
        W = jax.random.normal(k2, (64, in_feat), dtype=jnp.float32) * 0.02
        return {'x': x, 'W': W}
    _L0_tok_all = _L0_tok_setup()
    _L0_tok_in = {k: v for k, v in _L0_tok_all.items() if k in ('W',)}
    del _L0_tok_all

    def _L0_attn_setup():
        import jax, jax.numpy as jnp
        import numpy as np
        import math
        RADIUS = 32
        NUM_HEADS = 8
        B, L, DIM = (2, 2048, 64)
        key = jax.random.key(seed)
        k1, k2, k3, k4, k5 = jax.random.split(key, 5)
        s_in = 1.0 / math.sqrt(DIM)
        return {'x': jax.random.normal(k1, (B, L, DIM), dtype=jnp.float32), 'w_qkv': jax.random.normal(k2, (DIM, 3 * DIM), dtype=jnp.float32) * s_in, 'b_qkv': jax.random.normal(k3, (3 * DIM,), dtype=jnp.float32) * 0.01, 'w_proj': jax.random.normal(k4, (DIM, DIM), dtype=jnp.float32) * s_in, 'b_proj': jax.random.normal(k5, (DIM,), dtype=jnp.float32) * 0.01}
    _L0_attn_all = _L0_attn_setup()
    _L0_attn_in = {k: v for k, v in _L0_attn_all.items() if k in ('w_qkv', 'b_qkv', 'w_proj', 'b_proj')}
    del _L0_attn_all

    def _L0_ffn_setup():
        import math
        import jax, jax.numpy as jnp
        import numpy as np
        CAPACITY_FACTOR = 1.25
        key = jax.random.key(seed)
        ks = jax.random.split(key, 5)
        B, L, D, F, E = (8, 2048, 64, 256, 8)
        h = jax.random.normal(ks[0], (B, L, D), dtype=jnp.float32)
        gate_w = jax.random.normal(ks[1], (D, E), dtype=jnp.float32) * 0.02
        gate_b = jnp.zeros((E,), dtype=jnp.float32)
        w1 = jax.random.normal(ks[2], (E, D, F), dtype=jnp.float32) * (1.0 / math.sqrt(D))
        b1 = jnp.zeros((E, F), dtype=jnp.float32)
        w2 = jax.random.normal(ks[3], (E, F, D), dtype=jnp.float32) * (1.0 / math.sqrt(F))
        b2 = jnp.zeros((E, D), dtype=jnp.float32)
        return {'h': h, 'gate_w': gate_w, 'gate_b': gate_b, 'w1': w1, 'b1': b1, 'w2': w2, 'b2': b2}
    _L0_ffn_all = _L0_ffn_setup()
    _L0_ffn_in = {k: v for k, v in _L0_ffn_all.items() if k in ('gate_w', 'gate_b', 'w1', 'b1', 'w2', 'b2')}
    del _L0_ffn_all
    return {'x': x, 'L0_tok_W': _L0_tok_in['W'], 'L0_attn_w_qkv': _L0_attn_in['w_qkv'], 'L0_attn_b_qkv': _L0_attn_in['b_qkv'], 'L0_attn_w_proj': _L0_attn_in['w_proj'], 'L0_attn_b_proj': _L0_attn_in['b_proj'], 'L0_ffn_gate_w': _L0_ffn_in['gate_w'], 'L0_ffn_gate_b': _L0_ffn_in['gate_b'], 'L0_ffn_w1': _L0_ffn_in['w1'], 'L0_ffn_b1': _L0_ffn_in['b1'], 'L0_ffn_w2': _L0_ffn_in['w2'], 'L0_ffn_b2': _L0_ffn_in['b2']}

def reference(x, L0_tok_W, L0_attn_w_qkv, L0_attn_b_qkv, L0_attn_w_proj, L0_attn_b_proj, L0_ffn_gate_w, L0_ffn_gate_b, L0_ffn_w1, L0_ffn_b1, L0_ffn_w2, L0_ffn_b2):
    import jax
    import jax.numpy as jnp

    def _L0_tok_ref(x, W):
        import jax, jax.numpy as jnp
        import numpy as np
        PATCH_LEN = 16
        STRIDE = 8
        PAD = 8
        B, C, T, V = x.shape
        xp = jnp.pad(x, ((0, 0), (0, 0), (0, PAD), (0, 0)), mode='edge')
        Tp = T + PAD
        N = (Tp - PATCH_LEN) // STRIDE + 1
        idx = jnp.arange(N)[:, None] * STRIDE + jnp.arange(PATCH_LEN)[None, :]
        patches = xp[:, :, idx, :]
        patches = jnp.transpose(patches, (0, 4, 2, 3, 1))
        xf = jnp.fft.rfft(patches, axis=-2, norm='ortho')
        F = xf.shape[-2]
        x_real = xf.real.reshape(B, V, N, F * C)
        x_imag = xf.imag.reshape(B, V, N, F * C)
        x_emb = jnp.concatenate([x_real, x_imag], axis=-1)
        x_emb = x_emb @ W.T
        return x_emb.reshape(B, V * N, -1)

    def _L0_attn_ref(x, w_qkv, b_qkv, w_proj, b_proj):
        import jax, jax.numpy as jnp
        import numpy as np
        import math
        RADIUS = 32
        NUM_HEADS = 8
        B, L, DIM = (2, 2048, 64)
        B, L, dim = x.shape
        H = NUM_HEADS
        hd = dim // H
        R = RADIUS
        W = 2 * R + 1
        scale = math.sqrt(hd)
        qkv = x @ w_qkv + b_qkv
        qkv = qkv.reshape(B, L, 3, H, hd)
        qkv = jnp.transpose(qkv, (2, 0, 3, 1, 4))
        q = qkv[0].reshape(B * H, L, hd)
        k = qkv[1].reshape(B * H, L, hd)
        v = qkv[2].reshape(B * H, L, hd)
        k_p = jnp.pad(k, ((0, 0), (R, R), (0, 0)))
        v_p = jnp.pad(v, ((0, 0), (R, R), (0, 0)))
        idx = jnp.arange(L)[:, None] + jnp.arange(W)[None, :]
        k_w = k_p[:, idx]
        v_w = v_p[:, idx]
        scores = jnp.einsum('bld,blwd->blw', q, k_w) / scale
        attn = jax.nn.softmax(scores, axis=-1)
        out = jnp.einsum('blw,blwd->bld', attn, v_w)
        out = out.reshape(B, H, L, hd)
        out = jnp.transpose(out, (0, 2, 1, 3)).reshape(B, L, dim)
        return out @ w_proj + b_proj

    def _L0_ffn_ref(h, gate_w, gate_b, w1, b1, w2, b2):
        import math
        import jax, jax.numpy as jnp
        import numpy as np
        CAPACITY_FACTOR = 1.25
        B, L, D = h.shape
        E = gate_w.shape[1]
        T = B * L
        C = max(1, math.ceil(CAPACITY_FACTOR * T / E))
        x = h.reshape(T, D)
        logits = x @ gate_w + gate_b
        probs = jax.nn.softmax(logits, axis=-1)
        idx = jnp.argmax(probs, axis=-1)
        prb = jnp.take_along_axis(probs, idx[:, None], axis=1)[:, 0]
        one_hot = jax.nn.one_hot(idx, E, dtype=jnp.float32)
        pos = (jnp.cumsum(one_hot, axis=0) * one_hot).sum(-1).astype(jnp.int32) - 1
        kept = pos < C
        pos_safe = jnp.where(kept, pos, C)
        buf = jnp.zeros((E, C, D), dtype=h.dtype).at[idx, pos_safe].set(x, mode='drop')
        hmid = jax.nn.relu(jnp.einsum('ecd,edf->ecf', buf, w1) + b1[:, None, :])
        ybuf = jnp.einsum('ecf,efd->ecd', hmid, w2) + b2[:, None, :]
        pos_g = jnp.minimum(pos, C - 1)
        y_tok = ybuf[idx, pos_g] * (prb * kept)[:, None]
        y = y_tok.reshape(B, L, D)
        y = jnp.nan_to_num(y, nan=0.0, posinf=10000.0, neginf=-10000.0)
        return y
    h = _L0_tok_ref(x, L0_tok_W)
    h = _layernorm(h + _L0_attn_ref(h, L0_attn_w_qkv, L0_attn_b_qkv, L0_attn_w_proj, L0_attn_b_proj), axis=-1)
    h = _layernorm(h + _L0_ffn_ref(h, L0_ffn_gate_w, L0_ffn_gate_b, L0_ffn_w1, L0_ffn_b1, L0_ffn_w2, L0_ffn_b2), axis=-1)
    return h

_drawn_inputs = setup_inputs


def setup_inputs(seed=0):
    import zlib

    import numpy as np

    out = dict(_drawn_inputs(seed))
    spreads = {'L0_ffn_gate_b': (0.0, 0.1), 'L0_ffn_b1': (0.0, 0.8), 'L0_ffn_b2': (0.0, 0.656)}
    factors = {}
    for name, (base, spread) in spreads.items():
        noise = np.random.default_rng([zlib.crc32(name.encode()), seed]).standard_normal(out[name].shape)
        drawn = base * np.exp(spread * noise) if base else spread * noise
        out[name] = jnp.asarray(drawn.astype(out[name].dtype))
    for name, factor in factors.items():
        out[name] = (out[name] * factor).astype(out[name].dtype)
    return out
```

```python
from contextlib import ExitStack

import numpy as np

import concourse.bass as bass
from concourse import mybir

ALU = mybir.AluOpType
ACT = mybir.ActivationFunctionType
AX = mybir.AxisListType.X
F32 = mybir.dt.float32
BF16 = mybir.dt.bfloat16
I32 = mybir.dt.int32

P = 128
B, CH, TIME, V = 16, 64, 128, 64
PATCH, STRIDE = 16, 8
NP = TIME // STRIDE
L = V * NP
D = 64
F = PATCH // 2 + 1
NBLK = NP + 1
TT = STRIDE // 2
H, HD, R = 8, 8, 32
QT = 64
NT = L // QT
XP = L + 2 * R
G = 16
NG = L // G
GK = G + 2 * R
GC = 4
NC = NG // GC
QSTEPS = 4
TOK = L // P
E, FF = 8, 256
CAP = -(-5 * B * L // (4 * E))
SL = 512
NSTEP = CAP // SL
SI = SL // P
EPS = 1e-5
BIG = 1e30
VW = 16
QUADS = NT // 4

_widths = dict(ident=P, fold=D, keymask=2 * P, onehot=QT, winmask=GK, delta=G, before=P, sel=32,
               dft=PATCH, rev=E, unit=2, trash=TOK, heads=H)
COL, _at = {}, 0
for _n, _w in _widths.items():
    COL[_n] = (_at, _at + _w)
    _at += _w
NCONST = _at


def constants():
    c = np.zeros((P, NCONST), np.float32)

    def put(name, a, rows=slice(0, P)):
        c[rows, COL[name][0]:COL[name][0] + a.shape[1]] = a

    p = np.arange(P)
    put("ident", np.eye(P))
    put("fold", np.concatenate([np.eye(D)] * 2))
    key, j = np.arange(P)[None], np.arange(QT)[:, None]
    for odd in range(2):
        at = key if not odd else (key + QT) % P
        c[QT:, COL["keymask"][0] + odd * P:COL["keymask"][0] + (odd + 1) * P] = np.where(
            (at < j) | (at > j + 2 * R), -BIG, 0)
    put("onehot", np.eye(QT), slice(QT, P))
    kk, jj = np.arange(GK)[None], (p % G)[:, None]
    put("winmask", np.where((kk < jj) | (kk > jj + 2 * R), -BIG, 0))
    put("delta", (p % G)[:, None] == np.arange(G)[None])
    put("before", p[:, None] < p[None])
    put("sel", np.concatenate([(p // G)[:, None] == np.arange(16)[None],
                               (p // G)[:, None] + H == np.arange(16)[None]], 1))
    f, t = np.arange(F)[:, None], np.arange(PATCH)[None]
    angle = 2 * np.pi * ((f * t) % PATCH) / PATCH
    put("dft", np.concatenate([np.cos(angle), -np.sin(angle)]) / np.sqrt(PATCH), slice(0, 2 * F))
    put("heads", ((p % D) // HD)[:, None] == np.arange(H)[None])
    put("rev", np.broadcast_to(E - np.arange(E), (P, E)))
    put("unit", np.stack([np.where(p < D, HD ** -0.5, 1), 0 * p - 0.5], 1))
    put("trash", E * CAP + np.arange(TOK)[None] * P + p[:, None])
    return c


class Chain:

    def __init__(self, eng, sem):
        self.eng, self.sem, self.base, self.n = eng, sem, 0, 0

    def link(self, ins):
        self.n += 1
        ins.then_inc(self.sem, 1)
        self.eng.wait_ge(self.sem, self.base + self.n)

    def rebase(self, base):
        self.base, self.n = base, 0


def need(eng, sem, value):
    if not isinstance(value, int) or value > 0:
        eng.wait_ge(sem, value)


def build(nc, x, w_tok, w_qkv, b_qkv, w_proj, b_proj, gate_w, gate_b, w1, b1, w2, b2, consts, out):
    with ExitStack() as ctx:
        def sb(name, shape, dt=F32):
            return ctx.enter_context(nc.sbuf_tensor(name, shape, dt))

        def sem(name):
            return ctx.enter_context(nc.semaphore(name))

        slots = nc.dram_tensor("slots", [E * CAP + TOK * P, D], F32).ap()
        results = nc.dram_tensor("results", [E * CAP, D], F32).ap()

        cst = sb("cst", [P, NCONST])

        def const(name, rows=slice(0, P)):
            return cst[rows, COL[name][0]:COL[name][1]]

        ident = const("ident")
        before16 = sb("before16", [P, P], BF16)
        ones16 = sb("ones16", [P, P], BF16)
        sel16 = sb("sel16", [P, 32], BF16)
        wtok = sb("wtok", [P, TT, 2, D])
        wqk = sb("wqk", [P, 2 * D])
        wv = sb("wv", [P, D])
        wp = sb("wp", [D + 1, D])
        wg = sb("wg", [D + 1, E])
        qk_scale = cst[:, COL["unit"][0]:COL["unit"][0] + 1]
        minus_half = cst[:, COL["unit"][0] + 1:COL["unit"][0] + 2]
        qk_b = sb("qk_b", [P, 1])
        qk_bias = sb("qk_bias", [P, 1])
        vbias = sb("vbias", [P, TOK + 1, D])

        xt = sb("xt", [P, NBLK, TT, V])
        hcat = sb("hcat", [P, TOK + 1, P])
        qk32 = sb("qk32", [P, TOK + 1, P])
        qk_hi = sb("qk_hi", [P, XP], BF16)
        qk_lo = sb("qk_lo", [P, XP], BF16)
        q16 = sb("q16", [P, L], BF16)
        qd16 = sb("qd16", [P, NG, H, G], BF16)
        k16_hi = sb("k16_hi", [P, XP], BF16)
        k16_lo = sb("k16_lo", [P, XP], BF16)
        qd32 = sb("qd32", [P, H, L])
        kwin = sb("kwin", [P, NT, P])
        mneg = sb("mneg", [P, H, L], BF16)
        vals = [sb(f"vals{o}", [P, TOK, H, VW]) for o in range(2)]
        htok = sb("htok", [P, TOK, D])
        junk = sb("junk", [P, 2 * GC, GK])
        mx = sb("mx", [P, NG])
        mx_hi = sb("mx_hi", [P, NG], BF16)
        mx_rest = sb("mx_rest", [P, NG])
        mx_lo = sb("mx_lo", [P, NG], BF16)
        spread = [sb(f"spread{o}", [P, NG, G], BF16) for o in range(2)]
        mrow = sb("mrow", [2 * H, L], BF16)
        probs = sb("probs", [P, 3, H, QT])
        ot = sb("ot", [P, 2, 4, P])
        rden = sb("rden", [P, 2, 4, 4])
        atok = sb("atok", [P, TOK, D])
        aT = sb("aT", [D + 1, L])
        y = sb("y", [P, TOK, D])
        yc = sb("yc", [P, TOK, D])
        sq = sb("sq", [P, TOK, D])
        st = sb("st", [P, 8, TOK])
        h1 = sb("h1", [P, TOK, D])
        h1T = sb("h1T", [D + 1, L])
        h1_all = sb("h1_all", [P, B * TOK, D])
        wl = h1_all[0:2 * F, :, :].rearrange("r t d -> r (t d)").rearrange("r (d k c) -> r d k c", k=2, c=CH)
        lg = sb("lg", [P, TOK, E])
        ex = sb("ex", [P, TOK, E])
        cand = sb("cand", [P, TOK, E])
        oh16 = sb("oh16", [P, TOK + 1, E], BF16)
        posw = sb("posw", [P, TOK, E])
        rt = sb("rt", [P, 16, TOK])
        run = sb("run", [P, E])
        sidx = sb("sidx", [P, TOK], I32)
        gidx_all = sb("gidx_all", [P, B * TOK], I32)
        w_all = sb("w_all", [P, B * TOK])

        place = qd32[:, :, :].rearrange("p h q -> p (h q)")
        taken = [0]

        def again(width, rows=P):
            a = taken[0]
            taken[0] += width
            assert taken[0] <= H * L
            return place[0:rows, a:a + width]

        w1s = [again(FF, D + 1) for _ in range(2)]
        w2s = [again(2 * D).rearrange("p (f d) -> p f d", f=2) for _ in range(2)]
        b2s = [again(D) for _ in range(2)]
        xin = [again(SI * D).rearrange("p (i d) -> p i d", i=SI) for _ in range(2)]
        xinT = [again(SL, D + 1) for _ in range(2)]
        hid = [again(2 * SL).rearrange("p (f s) -> p f s", f=2) for _ in range(2)]
        yout = [again(SI * D).rearrange("p (i d) -> p i d", i=SI) for _ in range(2)]
        yg = again(2 * TOK * D).rearrange("p (k t d) -> p k t d", k=2, d=D)
        gidx = sb("gidx", [P, 2, TOK], I32)
        fin = again(2 * TOK * D).rearrange("p (k t d) -> p k t d", k=2, d=D)
        bad = again(TOK * D).rearrange("p (t d) -> p t d", d=D).bitcast(I32)

        ps = ctx.enter_context(nc.psum_tensor("ps", [P, 8, 512], F32))

        loaded = sem("loaded")
        dft_mm, w_ready, ready_v, ready_p, ready_a = (sem(n) for n in ("dft_mm", "w_ready", "ready_v", "ready_p", "ready_a"))
        zeroed = sem("zeroed")
        x_in, tok_mm, hcat_lo, hcat_hi = (sem(n) for n in ("x_in", "tok_mm", "hcat_lo", "hcat_hi"))
        qk_mm, qk_ev, parts_ok, kwin_ok = (sem(n) for n in ("qk_mm", "qk_ev", "parts_ok", "kwin_ok"))
        q16_in, k16_in, qd16_ok, q32_in, mneg_in = (sem(n) for n in ("q16_in", "k16_in", "qd16_ok", "q32_in", "mneg_in"))
        max_mm, max_rd, mx_ok, spread_ok, mrow_mm, mrow_ev = (
            sem(n) for n in ("max_mm", "max_rd", "mx_ok", "spread_ok", "mrow_mm", "mrow_ev"))
        vh_mm, v_ev, h_ev = (sem(n) for n in ("vh_mm", "v_ev", "h_ev"))
        score_mm, exp_ok, pv_mm, ot_ev, back_mm, norm_ok = (
            sem(n) for n in ("score_mm", "exp_ok", "pv_mm", "ot_ev", "back_mm", "norm_ok"))
        aT_mm, aT_ev, proj_mm, var_ok, rstd_ok, h1_ok = (
            sem(n) for n in ("aT_mm", "aT_ev", "proj_mm", "var_ok", "rstd_ok", "h1_ok"))
        h1T_mm, h1T_ev, gate_mm, gate_sub, gate_exp, oh_ok, cum_mm, idx_ok = (
            sem(n) for n in ("h1T_mm", "h1T_ev", "gate_mm", "gate_sub", "gate_exp", "oh_ok", "cum_mm", "idx_ok"))
        scattered, h1_saved = sem("scattered"), sem("h1_saved")
        dve_own = sem("dve_own")
        passed = sem("passed")
        w_in = [sem(f"w_in{i}") for i in range(2)]
        s_in = [sem(f"s_in{i}") for i in range(2)]
        xT_mm, xT_ev, l1_mm, hid_ev, l2_mm, y_ev = (sem(n) for n in ("xT_mm", "xT_ev", "l1_mm", "hid_ev", "l2_mm", "y_ev"))
        y_out = [sem(f"y_out{i}") for i in range(2)]
        gathered = [sem(f"gathered{i}") for i in range(2)]
        stored = [sem(f"stored{i}") for i in range(2)]
        gidx_ok, fvar_ok, frstd_ok, fin_ok = (sem(n) for n in ("gidx_ok", "fvar_ok", "frstd_ok", "fin_ok"))

        N_LOADS = 14
        xv = x.rearrange("b c (n f t) v -> b f c n (t v)", f=2, t=TT)
        outv = out.rearrange("b (t p) d -> b p t d", p=P)

        def apart(eng):
            eng.sem_inc(passed, 1)

        block = ctx.enter_context(nc.Block())

        @block.sync
        def _(sp):
            sp.dma_start(cst[:, :], consts).then_inc(loaded, 16)
            for k in range(2):
                sp.dma_start(wl[:, :, k, :], w_tok.rearrange("d (r c) -> r d c", c=CH)).then_inc(loaded, 16)
                half = slice(k * D, (k + 1) * D)
                sp.dma_start(wqk[half, :], w_qkv[:, 0:2 * D]).then_inc(loaded, 16)
                sp.dma_start(wv[half, :], w_qkv[:, 2 * D:3 * D]).then_inc(loaded, 16)
            sp.dma_start(wp[0:D, :], w_proj).then_inc(loaded, 16)
            sp.dma_start(wp[D:D + 1, :], b_proj.rearrange("(a d) -> a d", a=1)).then_inc(loaded, 16)
            sp.dma_start(wg[0:D, :], gate_w).then_inc(loaded, 16)
            sp.dma_start(wg[D:D + 1, :], gate_b.rearrange("(a d) -> a d", a=1)).then_inc(loaded, 16)
            sp.dma_start(qk_b[:, :], b_qkv[0:2 * D].rearrange("(p a) -> p a", a=1)).then_inc(loaded, 16)
            for k in range(2):
                sp.dma_start(vbias[:, k, :], b_qkv[2 * D:3 * D].partition_broadcast(P)).then_inc(loaded, 16)

            def load_x(b, dyn=None):
                for f in range(2):
                    half = slice(f * CH, (f + 1) * CH)
                    sp.dma_start(xt[half, 0:NP, :, :].rearrange("c n t v -> c n (t v)"), xv[b, f]).then_inc(x_in, 16)
                    sp.dma_start(xt[half, NP, :, :],
                                 x[b, :, TIME - 1:TIME, :].to_broadcast([CH, TT, V])).then_inc(x_in, 16)

            def place_front(b):
                sp.wait_ge(parts_ok, 2 * b + 2)
                for k, part in enumerate((qk_hi, qk_lo)):
                    half = slice(k * D, (k + 1) * D)
                    sp.dma_start(q16[half, :], part[0:D, R:R + L]).then_inc(q16_in, 16)
                for k in range(2):
                    half = slice(k * D, (k + 1) * D)
                    sp.dma_start(k16_hi[half, :], qk_hi[D:P, :]).then_inc(k16_in, 16)
                    sp.dma_start(k16_lo[half, :], qk_lo[D:P, :]).then_inc(k16_in, 16)
                q32 = qk32[:, :, :].rearrange("p t q -> p (t q)")
                for h in range(H):
                    rows = slice(h * HD, (h + 1) * HD)
                    sp.dma_start(qd32[rows, h, :], q32[rows, R:R + L]).then_inc(q32_in, 16)

            def place_maxima(b):
                sp.wait_ge(mrow_ev, b + 1)
                for k in range(2):
                    sp.dma_start(mneg[k:k + 1, :, :], mrow[k * H:(k + 1) * H, :]).then_inc(mneg_in, 16)

            def save_h1(b):
                sp.wait_ge(h1_ok, b + 1)
                sp.dma_start(h1_all[:, bass.ds(b * TOK, TOK), :], h1[:, :, :]).then_inc(h1_saved, 16)

            load_x(0)
            sp.wait_ge(ready_p, 2)
            zsrc = qd16[:, :, :, :].rearrange("p g h j -> p (g h j)").bitcast(F32)
            rows = (E * CAP) // 5 // P
            for k in range(5):
                sp.dma_start(slots[k * rows * P:(k + 1) * rows * P, :].rearrange("(p r) d -> p (r d)", p=P),
                             zsrc[:, 0:rows * D]).then_inc(zeroed, 16)
            sp.wait_ge(zeroed, 80)
            sp.wait_ge(ready_v, 1)
            sp.wait_ge(tok_mm, 1)
            load_x(1)
            place_front(0)
            place_maxima(0)

            def body(b, last=False):
                if last is False:
                    sp.wait_ge(tok_mm, b + 2)
                    if last is not None and not (isinstance(b, int) and b + 2 >= B):
                        load_x(b + 2)
                    place_front(b + 1)
                    place_maxima(b + 1)
                save_h1(b)

            body(0)
            with sp.Fori(1, B - 2) as b:
                body(b)
            body(B - 2)
            body(B - 1, last=True)

            sp.wait_ge(scattered, 16 * B * TOK)
            sp.wait_ge(q32_in, 128 * B)

            def experts(pair):
                for k in range(2):
                    e = pair * 2 + k
                    need(sp, y_ev, (pair * 2 + k - 1) * NSTEP)
                    sp.dma_start(w1s[k][0:D, :], w1[e]).then_inc(w_in[k], 16)
                    sp.dma_start(w1s[k][D:D + 1, :], b1[bass.ds(e, 1), :]).then_inc(w_in[k], 16)
                    sp.dma_start(w2s[k], w2[e].rearrange("(f p) d -> p f d", p=P)).then_inc(w_in[k], 16)
                    sp.dma_start(b2s[k], b2[e].partition_broadcast(P)).then_inc(w_in[k], 16)
                    for s in range(NSTEP):
                        n = k * NSTEP + s
                        step = pair * 2 * NSTEP + n
                        need(sp, xT_mm, step - 1)
                        sp.dma_start(xin[n % 2], slots[bass.ds((e * NSTEP + s) * SL, SL), :].rearrange(
                            "(p i) d -> p i d", i=SI)).then_inc(s_in[n % 2], 16)
                        if isinstance(step, int) and step == 0:
                            continue
                        sp.wait_ge(y_ev, step)
                        m = (n + 1) % 2
                        sp.dma_start(results[bass.ds((e * NSTEP + s - 1) * SL, SL), :].rearrange(
                            "(p i) d -> p i d", i=SI), yout[m]).then_inc(y_out[m], 16)

            experts(0)
            with sp.Fori(1, E // 2) as pair:
                experts(pair)
            sp.wait_ge(y_ev, E * NSTEP)
            sp.dma_start(results[E * CAP - SL:E * CAP, :].rearrange("(p i) d -> p i d", i=SI),
                         yout[1]).then_inc(y_out[1], 16)

            def store(b, k):
                sp.wait_ge(fin_ok, b + 1)
                sp.dma_start(outv[b], fin[:, k, :, :]).then_inc(stored[k], 16)

            with sp.Fori(0, B // 2) as pair:
                for k in range(2):
                    store(pair * 2 + k, k)
            for k in range(2):
                sp.wait_ge(stored[k], 16 * B // 2)

        @block.tensor
        def _(pe):
            mm = nc.tensor.matmul

            pe.wait_ge(loaded, 16 * N_LOADS)
            for d in range(D):
                i = mm(ps[:, d * PATCH // 512, d * PATCH % 512:d * PATCH % 512 + PATCH],
                       wl[:, d, :, :].rearrange("r k c -> r (k c)"), const("dft", slice(0, 2 * F)), start=True, stop=True)
            i.then_inc(dft_mm, 1)
            pe.wait_ge(w_ready, 4)
            pe.wait_ge(ready_v, 1)
            pe.wait_ge(ready_a, 2)

            def tokens(b):
                pe.wait_ge(x_in, 64 * b + 64)
                need(pe, h_ev, b)
                need(pe, v_ev, 5 * b)
                for k in range(2):
                    for t in range(TT):
                        mm(ps[:, 6 + k, :], wtok[:, t, :, :].rearrange("p s d -> p (s d)"),
                           xt[:, k * 8:(k + 1) * 8, t, :], start=(t == 0), stop=(t == TT - 1))
                need(pe, norm_ok, QUADS * b)
                for t in range(TT):
                    i = mm(ps[D:P, 5, 0:V], wtok[:, t, 1, :], xt[:, NP, t, :], start=(t == 0), stop=(t == TT - 1))
                i.then_inc(tok_mm, 1)

            hflat = hcat[:, :, :].rearrange("p t q -> p (t q)")

            def queries_keys(b):
                pe.wait_ge(hcat_lo, b + 1)
                pe.wait_ge(hcat_hi, 2 * b + 2)
                need(pe, mrow_ev, b)
                for k in range(2):
                    i = mm(ps[:, 2 + k, :], wqk[:, :], hflat[:, R + 512 * k:R + 512 * (k + 1)], start=True, stop=True)
                i.then_inc(qk_mm, 1)

            def maxima(b, c):
                if c == 0:
                    pe.wait_ge(qk_ev, b + 1)
                    pe.wait_ge(k16_in, 64 * b + 64)
                if c % (NC // QSTEPS) == 0:
                    pe.wait_ge(qd16_ok, QSTEPS * b + c // (NC // QSTEPS) + 1)
                if c >= 2:
                    pe.wait_ge(max_rd, NC * b + c - 1)
                for g in range(GC * c, GC * c + GC):
                    o = ps[:, 2 + c % 2, (g % GC) * GK:(g % GC + 1) * GK]
                    s = qd16[:, g, :, :].rearrange("p h j -> p (h j)")
                    mm(o, s, k16_hi[:, g * G:g * G + GK], start=True, stop=False)
                    i = mm(o, s, k16_lo[:, g * G:g * G + GK], start=False, stop=True)
                i.then_inc(max_mm, 1)

            def maxima_rows(b):
                pe.wait_ge(spread_ok, 2 * b + 2)
                pe.wait_ge(max_rd, NC * b + NC)
                for k in range(2):
                    for o in range(2):
                        i = mm(ps[0:2 * H, 2 + k, :], sel16[:, 16 * o:16 * o + 16],
                               spread[o][:, 32 * k:32 * (k + 1), :].rearrange("p g j -> p (g j)"),
                               start=(o == 0), stop=(o == 1))
                i.then_inc(mrow_mm, 1)

            def values(b):
                need(pe, gate_sub, b)
                need(pe, h1_ok, b)
                for t in range(TOK):
                    mm(ps[:, 6, t * D:(t + 1) * D], hcat[:, t, :], wv[:, :], start=True, stop=True)
                mm(ps[:, 4, 0:D], hcat[:, TOK, :], wv[:, :], start=True, stop=True)
                for t in range(TOK):
                    i = mm(ps[:, 7, t * D:(t + 1) * D], hflat[:, R + t * P:R + (t + 1) * P], const("fold"),
                           start=True, stop=True)
                i.then_inc(vh_mm, 1)

            def scores(b, t):
                if t == 0:
                    pe.wait_ge(kwin_ok, 4 * b + 4)
                    pe.wait_ge(q32_in, 128 * b + 128)
                    pe.wait_ge(mneg_in, 32 * b + 32)
                    need(pe, h1T_ev, b)
                if t >= 2:
                    pe.wait_ge(exp_ok, NT * b + t - 1)
                o = ps[:, t % 2, :]
                cols = slice(t * QT, (t + 1) * QT)
                mm(o, kwin[:, t, :], qd32[:, :, cols], start=True, stop=False)
                mm(o, ones16[:, :], mneg[:, :, cols], start=False, stop=True).then_inc(score_mm, 1)

            def weighted(b, t):
                if t == 0:
                    pe.wait_ge(v_ev, 5 * b + 5)
                if t % 4 == 0 and t:
                    pe.wait_ge(ot_ev, QUADS * b + t // 4)
                pe.wait_ge(exp_ok, NT * b + t + 1)
                for c in range(4):
                    i = mm(ps[32 * c:32 * c + 32, 4, (t % 4) * P:(t % 4 + 1) * P],
                           vals[t % 2][:, t // 2, 2 * c:2 * c + 2, :].rearrange("p h w -> p (h w)"),
                           probs[:, t % 3, 2 * c:2 * c + 2, :].rearrange("p h q -> p (h q)"), start=True, stop=True)
                i.then_inc(pv_mm, 1)

            def turn_back(b, k):
                pe.wait_ge(ot_ev, QUADS * b + k + 1)
                need(pe, norm_ok, QUADS * b + k)
                if k == 0:
                    need(pe, idx_ok, b)
                apart(pe)
                for s in range(4):
                    i = nc.tensor.transpose(ps[:, 5, s * P:(s + 1) * P], ot[:, k % 2, s, :], ident)
                i.then_inc(back_mm, 1)

            def attended_T(b):
                pe.wait_ge(norm_ok, QUADS * b + QUADS)
                pe.wait_ge(exp_ok, NT * b + NT)
                apart(pe)
                for t in range(TOK):
                    i = nc.tensor.transpose(ps[0:D, t // 4, (t % 4) * P:(t % 4 + 1) * P], atok[:, t, :], ident)
                i.then_inc(aT_mm, 1)

            def projection(b):
                pe.wait_ge(aT_ev, b + 1)
                for t in range(TOK):
                    i = mm(ps[:, 4, t * D:(t + 1) * D], aT[:, t * P:(t + 1) * P], wp[:, :], start=True, stop=True)
                i.then_inc(proj_mm, 1)

            def normed_T(b):
                pe.wait_ge(h1_ok, b + 1)
                apart(pe)
                for t in range(TOK):
                    i = nc.tensor.transpose(ps[0:D, t // 4, (t % 4) * P:(t % 4 + 1) * P], h1[:, t, :], ident)
                i.then_inc(h1T_mm, 1)

            def gate(b, front):
                pe.wait_ge(h1T_ev, b + 1)
                if front:
                    pe.wait_ge(hcat_lo, b + 2)
                    pe.wait_ge(hcat_hi, 2 * b + 4)
                for t in range(TOK):
                    i = mm(ps[:, 7, t * E:(t + 1) * E], h1T[:, t * P:(t + 1) * P], wg[:, :], start=True, stop=True)
                i.then_inc(gate_mm, 1)

            def counts(b):
                pe.wait_ge(oh_ok, b + 1)
                for s in range(1, TOK + 1):
                    mm(ps[:, 5, s * E:(TOK + 1) * E], ones16[:, :],
                       oh16[:, 0:TOK + 1 - s, :].rearrange("p t e -> p (t e)"),
                       start=(s == 1), stop=False, skip_group_check=True)
                mm(ps[:, 5, 0:TOK * E], before16[:, :], oh16[:, 0:TOK, :].rearrange("p t e -> p (t e)"),
                   start=False, stop=True, skip_group_check=True).then_inc(cum_mm, 1)

            def front(b):
                for c in range(NC):
                    maxima(b, c)

            tokens(0)
            queries_keys(0)
            front(0)
            maxima_rows(0)

            def body(b, last=False):
                values(b)
                for t in range(NT):
                    scores(b, t)
                    if t:
                        weighted(b, t - 1)
                    if t % 4 == 1 and t > 4:
                        turn_back(b, t // 4 - 1)
                weighted(b, NT - 1)
                if last:
                    turn_back(b, QUADS - 1)
                    attended_T(b)
                    projection(b)
                    normed_T(b)
                    gate(b, False)
                    counts(b)
                    return
                turn_back(b, QUADS - 1)
                tokens(b + 1)
                attended_T(b)
                projection(b)
                queries_keys(b + 1)
                for c in range(NC):
                    if c == NC // 2:
                        normed_T(b)
                    if c == NC // 2 + 3:
                        gate(b, True)
                    maxima(b + 1, c)
                counts(b)
                maxima_rows(b + 1)

            body(0)
            with pe.Fori(1, B - 1) as b:
                body(b)
            body(B - 1, last=True)

            pe.wait_ge(idx_ok, B)

            def turn(pair, n):
                step = pair * 2 * NSTEP + n
                uses = pair * NSTEP + n // 2
                pe.wait_ge(s_in[n % 2], 16 * uses + 16)
                need(pe, xT_ev, step - 1)
                apart(pe)
                for i in range(SI):
                    ins = nc.tensor.transpose(ps[0:D, n % 2, i * P:(i + 1) * P], xin[n % 2][:, i, :], ident)
                ins.then_inc(xT_mm, 1)

            def layer1(pair, n):
                step = pair * 2 * NSTEP + n
                k = n // NSTEP
                if n % NSTEP == 0:
                    pe.wait_ge(w_in[k], 64 * pair + 64)
                pe.wait_ge(xT_ev, step + 1)
                need(pe, hid_ev, 2 * (step - 1))
                for f in range(2):
                    i = mm(ps[:, 2 + 2 * (n % 2) + f, :], w1s[k][:, f * P:(f + 1) * P], xinT[n % 2], start=True, stop=True)
                i.then_inc(l1_mm, 1)

            def layer2(pair, n):
                step = pair * 2 * NSTEP + n
                k = n // NSTEP
                pe.wait_ge(hid_ev, 2 * step + 2)
                need(pe, y_ev, step - 1)
                for i in range(SI):
                    for f in range(2):
                        ins = mm(ps[:, 6 + n % 2, i * D:(i + 1) * D], hid[n % 2][:, f, i * P:(i + 1) * P],
                                 w2s[k][:, f, :], start=(f == 0), stop=(f == 1))
                ins.then_inc(l2_mm, 1)

            def experts(pair):
                turn(pair, 0)
                for n in range(2 * NSTEP):
                    layer1(pair, n)
                    if n + 1 < 2 * NSTEP:
                        turn(pair, n + 1)
                    layer2(pair, n)

            experts(0)
            with pe.Fori(1, E // 2) as pair:
                experts(pair)

        @block.scalar
        def _(act):
            act.wait_ge(loaded, 16 * N_LOADS)
            nc.scalar.activation(qk_bias[:, :], qk_b[:, :], ACT.Identity, scale=qk_scale).then_inc(ready_a, 1)
            nc.scalar.activation(sel16[:, :], const("sel"), ACT.Copy).then_inc(ready_a, 1)
            act.wait_ge(ready_a, 2)
            act.wait_ge(ready_v, 1)

            hflat = hcat[:, :, :].rearrange("p t q -> p (t q)")
            q32 = qk32[:, :, :].rearrange("p t q -> p (t q)")

            def tokens_low(b):
                act.wait_ge(tok_mm, b + 1)
                nc.scalar.activation(hflat[0:D, R:R + L].rearrange("p (v n) -> p v n", n=NP),
                                     ps[0:D, 6:8, :].rearrange("p k (n v) -> p v (k n)", v=V),
                                     ACT.Copy).then_inc(hcat_lo, 1)

            def queries_keys(b):
                act.wait_ge(qk_mm, b + 1)
                need(act, q32_in, 128 * b)
                need(act, kwin_ok, 4 * b)
                nc.scalar.activation(q32[:, R:R + L], ps[:, 2:4, :].rearrange("p k q -> p (k q)"), ACT.Identity,
                                     bias=qk_bias[:, :], scale=qk_scale).then_inc(qk_ev, 1)

            def maxima_rows(b):
                act.wait_ge(mrow_mm, b + 1)
                need(act, mneg_in, 32 * b)
                nc.scalar.activation(mrow[:, :], ps[0:2 * H, 2:4, :].rearrange("p k q -> p (k q)"),
                                     ACT.Copy).then_inc(mrow_ev, 1)

            def rows_back(b, k):
                act.wait_ge(pv_mm, NT * b + 4 * k + 4)
                need(act, back_mm, QUADS * b + k - 1)
                nc.scalar.activation(ot[:, k % 2, :, :].rearrange("p s c -> p (s c)"), ps[:, 4, :],
                                     ACT.Copy).then_inc(ot_ev, 1)

            tokens_low(0)
            queries_keys(0)
            maxima_rows(0)

            def body(b, last=False):
                act.wait_ge(vh_mm, b + 1)
                need(act, h1_ok, b)
                nc.scalar.activation(htok[:, :, :].rearrange("p t d -> p (t d)"), ps[:, 7, :], ACT.Copy).then_inc(h_ev, 1)
                for t in range(NT):
                    act.wait_ge(score_mm, NT * b + t + 1)
                    need(act, pv_mm, NT * b + t - 2)
                    nc.scalar.activation(probs[:, t % 3, :, :].rearrange("p h q -> p (h q)"), ps[:, t % 2, :],
                                         ACT.Exp).then_inc(exp_ok, 1)
                    if t % 4 == 0 and t:
                        rows_back(b, t // 4 - 1)
                rows_back(b, QUADS - 1)
                if not last:
                    tokens_low(b + 1)
                act.wait_ge(aT_mm, b + 1)
                need(act, proj_mm, b)
                nc.scalar.activation(aT[0:D, :], ps[0:D, 0:2, :].rearrange("p k q -> p (k q)"), ACT.Copy).then_inc(aT_ev, 1)
                if not last:
                    queries_keys(b + 1)
                act.wait_ge(h1T_mm, b + 1)
                need(act, gate_mm, b)
                nc.scalar.activation(h1T[0:D, :], ps[0:D, 0:2, :].rearrange("p k q -> p (k q)"), ACT.Copy).then_inc(h1T_ev, 1)
                act.wait_ge(gate_sub, b + 1)
                nc.scalar.activation(ex[:, :, :], lg[:, :, :], ACT.Exp).then_inc(gate_exp, 1)
                if not last:
                    maxima_rows(b + 1)

            body(0)
            with act.Fori(1, B - 1) as b:
                body(b)
            body(B - 1, last=True)

            def experts(pair):
                for n in range(2 * NSTEP):
                    step = pair * 2 * NSTEP + n
                    act.wait_ge(l1_mm, step + 1)
                    need(act, l2_mm, step - 1)
                    nc.scalar.activation(hid[n % 2][:, 0, :], ps[:, 2 + 2 * (n % 2), :], ACT.Relu).then_inc(hid_ev, 1)

            experts(0)
            with act.Fori(1, E // 2) as pair:
                experts(pair)

        @block.gpsimd
        def _(pool):
            nc.gpsimd.memset(qd16[:, :, :, :].rearrange("p g h j -> p (g h j)"), 0.0).then_inc(ready_p, 1)
            nc.gpsimd.memset(mneg[:, :, :].rearrange("p h q -> p (h q)"), 0.0).then_inc(ready_p, 1)
            pool.wait_ge(ready_v, 1)
            pool.wait_ge(loaded, 16 * N_LOADS)

            def diagonal(b):
                pool.wait_ge(q16_in, 32 * b + 32)
                need(pool, max_mm, NC * b)
                n = NG // QSTEPS
                for k in range(QSTEPS):
                    src = q16[:, k * n * G:(k + 1) * n * G].rearrange("p (g j) -> p g j", j=G)
                    nc.gpsimd.tensor_tensor(
                        qd16[:, k * n:(k + 1) * n, :, :], src.unsqueeze(2).to_broadcast([P, n, H, G]),
                        const("heads").unsqueeze(1).unsqueeze(3).to_broadcast([P, n, H, G]), ALU.mult
                    ).then_inc(qd16_ok, 1)

            def spread_maxima(b):
                need(pool, mrow_mm, b)
                for o, part in enumerate((mx_hi, mx_lo)):
                    pool.wait_ge(mx_ok, 2 * b + 1 + o)
                    nc.gpsimd.tensor_tensor(
                        spread[o][:, :, :], part[:, :].unsqueeze(2).to_broadcast([P, NG, G]),
                        const("delta").unsqueeze(1).to_broadcast([P, NG, G]), ALU.mult).then_inc(spread_ok, 1)

            def inv_std(src, dst, ready, done, n):
                pool.wait_ge(ready, n)
                nc.gpsimd.tensor_tensor(dst, src, minus_half.to_broadcast([P, TOK]), ALU.pow).then_inc(done, 1)

            def scatter(b):
                pool.wait_ge(idx_ok, b + 1)
                apart(pool)
                for t in range(TOK):
                    nc.gpsimd.indirect_dma_start(
                        out=slots, out_offset=bass.IndirectOffsetOnAxis(ap=sidx[:, t:t + 1], axis=0),
                        in_=h1[:, t, :], in_offset=None).then_inc(scattered, 16)

            pool.wait_ge(zeroed, 80)
            diagonal(0)
            spread_maxima(0)

            def body(b, last=False):
                if not last:
                    diagonal(b + 1)
                inv_std(st[:, 1, :], st[:, 2, :], var_ok, rstd_ok, b + 1)
                if not last:
                    spread_maxima(b + 1)
                scatter(b)

            body(0)
            with pool.Fori(1, B - 1) as b:
                body(b)
            body(B - 1, last=True)

            for m in range(2):
                pool.wait_ge(y_out[m], 16 * E * NSTEP // 2)

            def gather(pair):
                for k in range(2):
                    b = pair * 2 + k
                    pool.wait_ge(gidx_ok, b + 1)
                    need(pool, fin_ok, b - 1)
                    apart(pool)
                    for t in range(TOK):
                        nc.gpsimd.indirect_dma_start(
                            out=yg[:, k, t, :], out_offset=None, in_=results,
                            in_offset=bass.IndirectOffsetOnAxis(ap=gidx[:, k, t:t + 1], axis=0)).then_inc(gathered[k], 16)
                    if isinstance(b, int) and b == 0:
                        continue
                    inv_std(st[:, 1, :], st[:, 2, :], fvar_ok, frstd_ok, b)

            gather(0)
            with pool.Fori(1, B // 2) as pair:
                gather(pair)
            inv_std(st[:, 1, :], st[:, 2, :], fvar_ok, frstd_ok, B)

        @block.vector
        def _(dve):
            own = Chain(dve, dve_own)
            link = own.link
            v = nc.vector
            dve.wait_ge(loaded, 16 * N_LOADS)
            dve.wait_ge(ready_p, 2)

            link(v.memset(place[0:D, :], 0.0))
            link(v.tensor_copy(place[D:P, :].rearrange("p (n j) -> p n j", j=QT),
                               const("onehot", slice(D, P)).unsqueeze(1).to_broadcast([D, H * L // QT, QT])))
            for o in range(2):
                link(v.tensor_copy(kwin[D:P, :, :].rearrange("p (t o) k -> p o t k", o=2)[:, o],
                                   cst[D:P, COL["keymask"][0] + o * P:COL["keymask"][0] + (o + 1) * P]
                                   .unsqueeze(1).to_broadcast([D, NT // 2, P])))
                link(v.memset(vals[o][:, :, :, :].rearrange("p t h w -> p (t h w)"), 0.0))
                link(v.memset(vals[o][:, :, :, HD:HD + 1], 1.0))
            link(v.memset(hcat[:, :, :].rearrange("p t q -> p (t q)"), 0.0))
            link(v.memset(qk32[:, :, :].rearrange("p t q -> p (t q)"), 0.0))
            link(v.memset(aT[D:D + 1, :], 1.0))
            link(v.memset(h1T[D:D + 1, :], 1.0))
            link(v.memset(ones16[:, :], 1.0))
            link(v.tensor_copy(before16[:, :], const("before")))
            link(v.memset(oh16[:, :, :].rearrange("p t e -> p (t e)"), 0.0))
            link(v.memset(run[:, :], 0.0))
            for t in range(2, TOK + 1):
                link(v.tensor_copy(vbias[:, t, :], vbias[:, 1, :]))
            link(v.memset(vbias[0:R, 0, :], 0.0))
            link(v.memset(vbias[R:2 * R, TOK, :], 0.0))
            v.nop().then_inc(ready_v, 1)
            dve.wait_ge(dft_mm, 1)
            wps = ps[:, 0:2, :].rearrange("p k (d t) -> p (k d) t", t=PATCH)
            for f in range(2):
                half = slice(f * CH, (f + 1) * CH)
                for s in range(2):
                    t0 = s * STRIDE + f * TT
                    v.tensor_copy(wtok[half, :, s, :], wps[half, :, t0:t0 + TT].rearrange("p d t -> p t d")
                                  ).then_inc(w_ready, 1)

            hflat = hcat[:, :, :].rearrange("p t q -> p (t q)")
            q32 = qk32[:, :, :].rearrange("p t q -> p (t q)")

            def tokens_high(b):
                dve.wait_ge(tok_mm, b + 1)
                hv = hflat[D:P, R:R + L].rearrange("p (v n) -> p v n", n=NP)
                v.tensor_copy(hv[:, :, 0:NP - 1],
                              ps[D:P, 6:8, :].rearrange("p k (n v) -> p v (k n)", v=V)[:, :, 1:NP]).then_inc(hcat_hi, 1)
                v.tensor_copy(hv[:, :, NP - 1:NP], ps[D:P, 5, 0:V].unsqueeze(2)).then_inc(hcat_hi, 1)

            def parts(b):
                dve.wait_ge(qk_ev, b + 1)
                need(dve, q16_in, 32 * b)
                need(dve, k16_in, 64 * b)
                v.tensor_copy(qk_hi[:, :], q32[:, 0:XP]).then_inc(parts_ok, 1)
                dve.wait_ge(parts_ok, 2 * b + 1)
                v.tensor_tensor(qk_lo[:, :], q32[:, 0:XP], qk_hi[:, :], ALU.subtract).then_inc(parts_ok, 1)
                kw = kwin[0:D, :, :].rearrange("p (t o) (f k) -> p o f t k", o=2, f=2)
                for o, f, t0, f0 in ((0, 0, 0, 0), (0, 1, 0, 1), (1, 1, 0, 1), (1, 0, 1, 0)):
                    v.tensor_copy(kw[:, o, f], qk32[D:P, t0:t0 + TOK, f0 * QT:(f0 + 1) * QT]).then_inc(kwin_ok, 1)

            def maxima(b, c):
                need(dve, max_rd, NC * b + c - 1)
                dve.wait_ge(max_mm, NC * b + c + 1)
                apart(dve)
                for g in range(GC * c, GC * c + GC):
                    s = ps[:, 2 + c % 2, (g % GC) * GK:(g % GC + 1) * GK]
                    i = v.tensor_tensor_reduce(junk[:, g % (2 * GC), :], s, const("winmask"), 1.0, -3e38,
                                               ALU.add, ALU.max, mx[:, g:g + 1])
                i.then_inc(max_rd, 1)

            def maxima_parts(b):
                dve.wait_ge(max_rd, NC * b + NC)
                need(dve, spread_ok, 2 * b)
                v.tensor_scalar(mx_hi[:, :], mx[:, :], -1.0, None, ALU.mult).then_inc(mx_ok, 1)
                dve.wait_ge(mx_ok, 2 * b + 1)
                link(v.tensor_tensor(mx_rest[:, :], mx[:, :], mx_hi[:, :], ALU.add))
                v.tensor_scalar(mx_lo[:, :], mx_rest[:, :], -1.0, None, ALU.mult).then_inc(mx_ok, 1)

            def values(b):
                dve.wait_ge(vh_mm, b + 1)
                pv = ps[:, 6, :].rearrange("p (t h d) -> p t h d", h=H, d=HD)
                p9 = ps[:, 4, 0:D].rearrange("p (t h d) -> p t h d", t=1, d=HD)
                vb = vbias[:, :, :].rearrange("p t (h d) -> p t h d", d=HD)
                e, o = (u[:, :, :, 0:HD] for u in vals)
                v.tensor_tensor(e, pv, vb[:, 0:TOK], ALU.add).then_inc(v_ev, 1)
                v.tensor_tensor(o[D:P], pv[D:P], vb[D:P, 0:TOK], ALU.add).then_inc(v_ev, 1)
                v.tensor_tensor(o[0:D, 0:TOK - 1], pv[0:D, 1:TOK], vb[0:D, 1:TOK], ALU.add).then_inc(v_ev, 1)
                v.tensor_tensor(o[0:D, TOK - 1:TOK], p9[0:D], vb[0:D, TOK:TOK + 1], ALU.add).then_inc(v_ev, 2)

            def normalize(b, k):
                dve.wait_ge(back_mm, QUADS * b + k + 1)
                bank = ps[:, 5, :].rearrange("p (s c h w) -> p s c h w", s=4, c=4, h=2)
                for hh in range(2):
                    half = slice(hh * D, (hh + 1) * D)
                    i = v.reciprocal(rden[half, k % 2, :, :], bank[half, :, :, hh, HD])
                link(i)
                at = atok[:, :, :].rearrange("p t (c h d) -> p t c h d", c=4, h=2)
                for hh in range(2):
                    half = slice(hh * D, (hh + 1) * D)
                    for s in range(4):
                        i = v.tensor_tensor(
                            at[(s % 2) * D:(s % 2 + 1) * D, 2 * k + s // 2, :, hh, :], bank[half, s, :, hh, 0:HD],
                            rden[half, k % 2, s, :].unsqueeze(2).to_broadcast([D, 4, HD]), ALU.mult)
                i.then_inc(norm_ok, 1)

            def bc(a, n):
                return a.unsqueeze(2).to_broadcast([P, TOK, n])

            def norm_stats(src, ready):
                link(v.tensor_reduce(st[:, 0, :], src, AX, ALU.add))
                link(v.tensor_scalar(st[:, 3, :], st[:, 0, :], 1.0 / D, None, ALU.mult))
                link(v.tensor_tensor(yc[:, :, :], src, bc(st[:, 3, :], D), ALU.subtract))
                link(v.tensor_tensor(sq[:, :, :], yc[:, :, :], yc[:, :, :], ALU.mult))
                link(v.tensor_reduce(st[:, 4, :], sq[:, :, :], AX, ALU.add))
                v.tensor_scalar(st[:, 1, :], st[:, 4, :], 1.0 / D, EPS, ALU.mult, ALU.add).then_inc(ready, 1)

            def first_norm(b):
                dve.wait_ge(proj_mm, b + 1)
                dve.wait_ge(h_ev, b + 1)
                link(v.tensor_tensor(y[:, :, :].rearrange("p t d -> p (t d)"), ps[:, 4, :],
                                     htok[:, :, :].rearrange("p t d -> p (t d)"), ALU.add))
                norm_stats(y[:, :, :], var_ok)
                dve.wait_ge(rstd_ok, b + 1)
                need(dve, scattered, 16 * TOK * b)
                need(dve, h1_saved, 16 * b)
                v.tensor_tensor(h1[:, :, :], yc[:, :, :], bc(st[:, 2, :], D), ALU.mult).then_inc(h1_ok, 1)

            def route(b):
                dve.wait_ge(gate_mm, b + 1)
                logits = ps[:, 7, 0:TOK * E].rearrange("p (t e) -> p t e", e=E)
                lmax, esum, prb, code, pos, ebase, kept, t0, t1, t2 = (rt[:, k, :] for k in range(10))
                link(v.tensor_reduce(lmax, logits, AX, ALU.max))
                v.tensor_tensor(lg[:, :, :], logits, bc(lmax, E), ALU.subtract).then_inc(gate_sub, 1)
                dve.wait_ge(gate_sub, b + 1)
                link(v.tensor_scalar(cand[:, :, :], lg[:, :, :], 0.0, None, ALU.is_ge))
                link(v.tensor_tensor(cand[:, :, :], cand[:, :, :],
                                     const("rev").unsqueeze(1).to_broadcast([P, TOK, E]), ALU.mult))
                link(v.tensor_reduce(code, cand[:, :, :], AX, ALU.max))
                v.tensor_tensor(oh16[:, 0:TOK, :], cand[:, :, :], bc(code, E), ALU.is_equal).then_inc(oh_ok, 1)
                dve.wait_ge(gate_exp, b + 1)
                link(v.tensor_reduce(esum, ex[:, :, :], AX, ALU.add))
                link(v.reciprocal(prb, esum))
                dve.wait_ge(oh_ok, b + 1)
                dve.wait_ge(cum_mm, b + 1)
                cnt = ps[:, 5, 0:(TOK + 1) * E].rearrange("p (t e) -> p t e", e=E)
                link(v.tensor_tensor(posw[:, :, :], cnt[:, 0:TOK, :],
                                     run[:, :].unsqueeze(1).to_broadcast([P, TOK, E]), ALU.add))
                link(v.tensor_tensor(posw[:, :, :], posw[:, :, :], oh16[:, 0:TOK, :], ALU.mult))
                link(v.tensor_reduce(pos, posw[:, :, :], AX, ALU.add))
                link(v.tensor_tensor(run[:, :], cnt[:, TOK, :], run[:, :], ALU.add))
                link(v.tensor_scalar(ebase, code, float(-CAP), float(E * CAP), ALU.mult, ALU.add))
                link(v.tensor_scalar(kept, pos, float(CAP), None, ALU.is_lt))
                link(v.tensor_tensor(t0, ebase, pos, ALU.add))
                link(v.tensor_tensor(t0, t0, const("trash"), ALU.subtract))
                link(v.tensor_tensor(t0, t0, kept, ALU.mult))
                v.tensor_tensor(sidx[:, :], t0, const("trash"), ALU.add).then_inc(idx_ok, 1)
                link(v.tensor_scalar(t1, pos, float(CAP - 1), None, ALU.min))
                cols = bass.ds(b * TOK, TOK)
                link(v.tensor_tensor(gidx_all[:, cols], t1, ebase, ALU.add))
                link(v.tensor_tensor(w_all[:, cols], prb, kept, ALU.mult))

            tokens_high(0)
            parts(0)
            for c in range(NC):
                maxima(0, c)
            maxima_parts(0)

            def body(b, last=False):
                values(b)
                for k in range(QUADS):
                    normalize(b, k)
                if not last:
                    tokens_high(b + 1)
                    parts(b + 1)
                first_norm(b)
                if not last:
                    for c in range(NC):
                        maxima(b + 1, c)
                    maxima_parts(b + 1)
                route(b)

            start = own.n
            body(0)
            per_image = own.n - start
            with dve.Fori(1, B - 1) as b:
                own.rebase(start + b * per_image)
                body(b)
            own.rebase(start + (B - 1) * per_image)
            body(B - 1, last=True)

            for k in range(2):
                link(v.memset(xinT[k][D:D + 1, :], 1.0))

            def turned(pair, n):
                step = pair * 2 * NSTEP + n
                dve.wait_ge(xT_mm, step + 1)
                need(dve, l1_mm, step - 1)
                v.tensor_copy(xinT[n % 2][0:D, :], ps[0:D, n % 2, :]).then_inc(xT_ev, 1)

            def experts(pair):
                turned(pair, 0)
                for n in range(2 * NSTEP):
                    step = pair * 2 * NSTEP + n
                    dve.wait_ge(l1_mm, step + 1)
                    need(dve, l2_mm, step - 1)
                    v.tensor_scalar(hid[n % 2][:, 1, :], ps[:, 3 + 2 * (n % 2), :], 0.0, None, ALU.max).then_inc(hid_ev, 1)
                    if n + 1 < 2 * NSTEP:
                        turned(pair, n + 1)
                    dve.wait_ge(l2_mm, step + 1)
                    need(dve, y_out[n % 2], 16 * (pair * NSTEP + n // 2))
                    v.tensor_tensor(yout[n % 2], ps[:, 6 + n % 2, 0:SI * D].rearrange("p (i d) -> p i d", i=SI),
                                    b2s[n // NSTEP].unsqueeze(1).to_broadcast([P, SI, D]), ALU.add).then_inc(y_ev, 1)

            experts(0)
            with dve.Fori(1, E // 2) as pair:
                experts(pair)

            dve.wait_ge(h1_saved, 16 * B)

            def indices(b, k):
                v.tensor_copy(gidx[:, k, :], gidx_all[:, bass.ds(b * TOK, TOK)]).then_inc(gidx_ok, 1)

            def finish(pair, k):
                b = pair * 2 + k
                dve.wait_ge(gathered[k], 16 * TOK * (pair + 1))
                g = yg[:, k, :, :]
                cols = bass.ds(b * TOK, TOK)
                link(v.tensor_tensor(g, g, bc(w_all[:, cols], D), ALU.mult))
                link(v.tensor_scalar(bad[:, :, :], g, 0.0, 0.0, ALU.mult, ALU.not_equal))
                link(v.tensor_scalar(sq[:, :, :], g, -1e4, 1e4, ALU.max, ALU.min))
                link(v.tensor_tensor(y[:, :, :], g, g, ALU.is_equal))
                link(v.tensor_tensor(sq[:, :, :], sq[:, :, :], y[:, :, :], ALU.mult))
                apart(dve)
                link(v.copy_predicated(g, bad[:, :, :], sq[:, :, :]))
                link(v.tensor_tensor(y[:, :, :], g, h1_all[:, cols, :], ALU.add))
                norm_stats(y[:, :, :], fvar_ok)
                dve.wait_ge(frstd_ok, b + 1)
                need(dve, stored[k], 16 * pair)
                v.tensor_tensor(fin[:, k, :, :], yc[:, :, :], bc(st[:, 2, :], D), ALU.mult).then_inc(fin_ok, 1)

            indices(0, 0)
            indices(1, 1)

            def finish_pair(pair, more):
                for k in range(2):
                    finish(pair, k)
                    if more:
                        indices(pair * 2 + k + 2, k)

            start = own.n
            base = own.base
            finish_pair(0, True)
            per_pair = own.n - start
            with dve.Fori(1, B // 2 - 1) as pair:
                own.rebase(base + start + pair * per_pair)
                finish_pair(pair, True)
            own.rebase(base + start + (B // 2 - 1) * per_pair)
            finish_pair(B // 2 - 1, False)


_INS = ["x", "L0_tok_W", "L0_attn_w_qkv", "L0_attn_b_qkv", "L0_attn_w_proj", "L0_attn_b_proj", "L0_ffn_gate_w",
        "L0_ffn_gate_b", "L0_ffn_w1", "L0_ffn_b1", "L0_ffn_w2", "L0_ffn_b2"]


def kernel(**inputs):
    import concourse.bacc as _bacc
    from concourse.bass_utils import run_bass_kernel_spmd as _run

    nc = _bacc.Bacc("TRN2", target_bir_lowering=False, num_devices=1)
    arrays, args = {}, []
    for name in _INS:
        a = np.ascontiguousarray(inputs[name])
        arrays[f"in_{name}"] = a
        args.append(nc.dram_tensor(f"in_{name}", a.shape, mybir.dt.from_np(a.dtype), kind="ExternalInput").ap())
    arrays["in_consts"] = constants()
    args.append(nc.dram_tensor("in_consts", (P, NCONST), F32, kind="ExternalInput").ap())
    args.append(nc.dram_tensor("out_0", (B, L, D), F32, kind="ExternalOutput").ap())
    build(nc, *args)
    r = _run(nc, [arrays], core_ids=[0])
    return r.results[0]["out_0"]
```

```python
from contextlib import ExitStack

import numpy as np

import concourse.bass as bass
from concourse import mybir

ALU = mybir.AluOpType
ACT = mybir.ActivationFunctionType
AX = mybir.AxisListType.X
F32 = mybir.dt.float32
BF16 = mybir.dt.bfloat16
I32 = mybir.dt.int32

P = 128
B, CH, TIME, V = 16, 64, 128, 64
PATCH, STRIDE = 16, 8
NP = TIME // STRIDE
L = V * NP
D = 64
F = PATCH // 2 + 1
NBLK = NP + 1
TT = STRIDE // 2
H, HD, R = 8, 8, 32
QT = 64
NT = L // QT
XP = L + 2 * R
G = 32
NG = L // G
GK = G + 2 * R
HG, HW = 2, 4
GC = 2
NC = NG // GC
QSTEPS = 4
TOK = L // P
E, FF = 8, 256
CAP = -(-5 * B * L // (4 * E))
SL = 512
NSTEP = CAP // SL
SI = SL // P
EPS = 1e-5
LINKS = 29
BIG = 1e30
VW = 16
CNT = TOK * E
CHUNK_TILE = 10
QUADS = NT // 4

_widths = dict(ident=P, fold=D, keymask=2 * P, onehot=QT, winmask=GK, delta=G, before=P, sel=4 * 16,
               dft=PATCH, rev=E, unit=2, trash=TOK, heads=HW)
COL, _at = {}, 0
for _n, _w in _widths.items():
    COL[_n] = (_at, _at + _w)
    _at += _w
NCONST = _at


def constants():
    c = np.zeros((P, NCONST), np.float32)

    def put(name, a, rows=slice(0, P)):
        c[rows, COL[name][0]:COL[name][0] + a.shape[1]] = a

    p = np.arange(P)
    put("ident", np.eye(P))
    put("fold", np.concatenate([np.eye(D)] * 2))
    key, j = np.arange(P)[None], np.arange(QT)[:, None]
    for odd in range(2):
        at = key if not odd else (key + QT) % P
        c[QT:, COL["keymask"][0] + odd * P:COL["keymask"][0] + (odd + 1) * P] = np.where(
            (at < j) | (at > j + 2 * R), -BIG, 0)
    put("onehot", np.eye(QT), slice(QT, P))
    kk, jj = np.arange(GK)[None], (p % G)[:, None]
    put("winmask", np.where((kk < jj) | (kk > jj + 2 * R), -BIG, 0))
    put("delta", (p % G)[:, None] == np.arange(G)[None])
    put("before", p[:, None] < p[None])
    put("sel", np.concatenate([(p // G)[:, None] + H * o + HW * g == np.arange(16)[None]
                               for o in range(2) for g in range(HG)], 1))
    f, t = np.arange(F)[:, None], np.arange(PATCH)[None]
    angle = 2 * np.pi * ((f * t) % PATCH) / PATCH
    put("dft", np.concatenate([np.cos(angle), -np.sin(angle)]) / np.sqrt(PATCH), slice(0, 2 * F))
    put("heads", ((p % (P // 4)) // HD)[:, None] == np.arange(HW)[None])
    put("rev", np.broadcast_to(E - np.arange(E), (P, E)))
    put("unit", np.stack([np.where(p < D, HD ** -0.5, 1), 0 * p - 0.5], 1))
    put("trash", E * CAP + np.arange(TOK)[None] * P + p[:, None])
    return c


class Chain:

    def __init__(self, eng, sem):
        self.eng, self.sem, self.base, self.n = eng, sem, 0, 0

    def link(self, ins):
        self.n += 1
        ins.then_inc(self.sem, 1)
        self.eng.wait_ge(self.sem, self.base + self.n)

    def rebase(self, base):
        self.base, self.n = base, 0


def need(eng, sem, value):
    if not isinstance(value, int) or value > 0:
        eng.wait_ge(sem, value)


def build(nc, x, w_tok, w_qkv, b_qkv, w_proj, b_proj, gate_w, gate_b, w1, b1, w2, b2, consts, out):
    with ExitStack() as ctx:
        def sb(name, shape, dt=F32):
            return ctx.enter_context(nc.sbuf_tensor(name, shape, dt))

        def sem(name):
            return ctx.enter_context(nc.semaphore(name))

        slots = nc.dram_tensor("slots", [E * CAP + TOK * P, D], F32).ap()
        results = nc.dram_tensor("results", [E * CAP, D], F32).ap()

        cst = sb("cst", [P, NCONST])

        def const(name, rows=slice(0, P)):
            return cst[rows, COL[name][0]:COL[name][1]]

        ident = const("ident")
        before16 = sb("before16", [P, P], BF16)
        ones16 = sb("ones16", [P, P], BF16)
        sel16 = sb("sel16", [P, 64], BF16)
        wtok = sb("wtok", [P, TT, 2, D])
        wqk = sb("wqk", [P, 2 * D])
        wv = sb("wv", [P, D])
        wp2 = sb("wp2", [P, 2, D])
        bp2 = sb("bp2", [P, 1])
        bv2 = sb("bv2", [P, 1])
        wg2 = sb("wg2", [P, 2, E])
        bg2 = sb("bg2", [P, E])
        qk_scale = cst[:, COL["unit"][0]:COL["unit"][0] + 1]
        minus_half = cst[:, COL["unit"][0] + 1:COL["unit"][0] + 2]
        qk_b = sb("qk_b", [P, 1])
        qk_bias = sb("qk_bias", [P, 1])
        xt = sb("xt", [P, NBLK, TT, V])
        hcat = sb("hcat", [P, TOK + 1, P])
        qk32 = sb("qk32", [P, TOK + 1, P])
        qk_hi = sb("qk_hi", [P, XP], BF16)
        qk_lo = sb("qk_lo", [P, XP], BF16)
        q16 = sb("q16", [P, HG, L], BF16)
        k16 = sb("k16", [P, HG, XP], BF16)
        qd16 = sb("qd16", [P, NG, HG, HW, G], BF16)
        qd32 = sb("qd32", [P, H, L])
        kwin = sb("kwin", [P, NT, P])
        mneg = sb("mneg", [P, H, L], BF16)
        vals = [sb(f"vals{o}", [P, TOK, H, VW]) for o in range(2)]
        vT = sb("vT", [P, TOK // 2, P])
        vT_last = sb("vT_last", [D, P])
        hT = sb("hT", [P, TOK // 2 * P])
        junk = sb("junk", [P, 2 * GC * HG, GK])
        mx = sb("mx", [P, 2, HG, NG // 2])
        mx_hi = sb("mx_hi", [P, 2, HG, NG // 2], BF16)
        mx_rest = sb("mx_rest", [P, 2, HG, NG // 2])
        mx_lo = sb("mx_lo", [P, 2, HG, NG // 2], BF16)
        spread = [sb(f"spread{o}", [P, 2, HG * NG // 2, G], BF16) for o in range(2)]
        mrow = sb("mrow", [2 * H, L], BF16)
        probs = sb("probs", [P, 3, H, QT])
        ot = sb("ot", [P, 2, 4, P])
        rden = sb("rden", [P, 2, 4, 4])
        atok = sb("atok", [P, TOK, D])
        aT = sb("aT", [P, L // 2])
        yT = sb("yT", [P, L // 2])
        y = sb("y", [P, TOK, D])
        yc = sb("yc", [P, TOK, D])
        sq = sb("sq", [P, TOK, D])
        st = sb("st", [P, 8, TOK])
        h1 = sb("h1", [P, TOK, D])
        h1T = sb("h1T", [P, L // 2])
        lgT = sb("lgT", [2 * E, L // 2])
        h1_all = sb("h1_all", [P, B * TOK, D])
        wl = h1_all[0:2 * F, :, :].rearrange("r t d -> r (t d)").rearrange("r (d k c) -> r d k c", k=2, c=CH)
        logit = sb("logit", [P, TOK, E])
        lg = sb("lg", [P, TOK, E])
        ex = sb("ex", [P, TOK, E])
        cand = sb("cand", [P, TOK, E])
        oh16 = sb("oh16", [P, TOK + 1, E], BF16)
        posw = sb("posw", [P, TOK, E])
        rt = sb("rt", [P, 16, TOK])
        run = sb("run", [P, E])
        sidx = sb("sidx", [P, TOK], I32)
        gidx_all = sb("gidx_all", [P, B * TOK], I32)
        w_all = sb("w_all", [P, B * TOK])

        place = qd32[:, :, :].rearrange("p h q -> p (h q)")
        taken = [0]

        def again(width, rows=P):
            a = taken[0]
            taken[0] += width
            assert taken[0] <= H * L
            return place[0:rows, a:a + width]

        w1s = [again(FF, D + 1) for _ in range(2)]
        w2s = [again(2 * D).rearrange("p (f d) -> p f d", f=2) for _ in range(2)]
        b2s = [again(D) for _ in range(2)]
        xin = [again(SI * D).rearrange("p (i d) -> p i d", i=SI) for _ in range(2)]
        xinT = [again(SL, D + 1) for _ in range(2)]
        hid = [again(2 * SL).rearrange("p (f s) -> p f s", f=2) for _ in range(2)]
        yout = [again(SI * D).rearrange("p (i d) -> p i d", i=SI) for _ in range(2)]
        yg = again(2 * TOK * D).rearrange("p (k t d) -> p k t d", k=2, d=D)
        gidx = sb("gidx", [P, 2, TOK], I32)
        fin = again(2 * TOK * D).rearrange("p (k t d) -> p k t d", k=2, d=D)
        bad = again(TOK * D).rearrange("p (t d) -> p t d", d=D).bitcast(I32)

        ps = ctx.enter_context(nc.psum_tensor("ps", [P, 8, 512], F32))

        loaded = sem("loaded")
        dft_mm, w_ready, ready_v, ready_p, ready_a = (sem(n) for n in ("dft_mm", "w_ready", "ready_v", "ready_p", "ready_a"))
        zeroed = sem("zeroed")
        x_in, tok_mm, hcat_lo, hcat_hi = (sem(n) for n in ("x_in", "tok_mm", "hcat_lo", "hcat_hi"))
        qk_mm, qk_ev, parts_ok, kwin_ok = (sem(n) for n in ("qk_mm", "qk_ev", "parts_ok", "kwin_ok"))
        q16_in, k16_in, qd16_ok, q32_in, mneg_in = (sem(n) for n in ("q16_in", "k16_in", "qd16_ok", "q32_in", "mneg_in"))
        max_mm, max_rd, mx_ok, spread_ok, mrow_mm, mrow_ev = (
            sem(n) for n in ("max_mm", "max_rd", "mx_ok", "spread_ok", "mrow_mm", "mrow_ev"))
        vh_mm, vT_ev, h_ev, vback_mm, v_ev = (sem(n) for n in ("vh_mm", "vT_ev", "h_ev", "vback_mm", "v_ev"))
        yT_ev, yback_mm, centred, lgT_ev, gback_mm = (sem(n) for n in ("yT_ev", "yback_mm", "centred", "lgT_ev", "gback_mm"))
        score_mm, exp_ok, pv_mm, ot_ev, back_mm, norm_ok = (
            sem(n) for n in ("score_mm", "exp_ok", "pv_mm", "ot_ev", "back_mm", "norm_ok"))
        aT_mm, aT_ev, proj_mm, var_ok, rstd_ok, h1_ok = (
            sem(n) for n in ("aT_mm", "aT_ev", "proj_mm", "var_ok", "rstd_ok", "h1_ok"))
        h1T_mm, h1T_ev, gate_mm, gate_sub, gate_exp, oh_ok, cum_mm, idx_ok = (
            sem(n) for n in ("h1T_mm", "h1T_ev", "gate_mm", "gate_sub", "gate_exp", "oh_ok", "cum_mm", "idx_ok"))
        scattered, h1_saved = sem("scattered"), sem("h1_saved")
        dve_own = sem("dve_own")
        passed = sem("passed")
        w_in = [sem(f"w_in{i}") for i in range(2)]
        s_in = [sem(f"s_in{i}") for i in range(2)]
        xT_mm, xT_ev, l1_mm, hid_ev, l2_mm, y_ev = (sem(n) for n in ("xT_mm", "xT_ev", "l1_mm", "hid_ev", "l2_mm", "y_ev"))
        y_out = [sem(f"y_out{i}") for i in range(2)]
        gathered = [sem(f"gathered{i}") for i in range(2)]
        stored = [sem(f"stored{i}") for i in range(2)]
        gidx_ok, fvar_ok, frstd_ok, fin_ok = (sem(n) for n in ("gidx_ok", "fvar_ok", "frstd_ok", "fin_ok"))

        N_LOADS = 17
        xv = x.rearrange("b c (n f t) v -> b f c n (t v)", f=2, t=TT)
        outv = out.rearrange("b (t p) d -> b p t d", p=P)

        def apart(eng):
            eng.sem_inc(passed, 1)

        block = ctx.enter_context(nc.Block())

        @block.sync
        def _(sp):
            sp.dma_start(cst[:, :], consts).then_inc(loaded, 16)
            for k in range(2):
                sp.dma_start(wl[:, :, k, :], w_tok.rearrange("d (r c) -> r d c", c=CH)).then_inc(loaded, 16)
                half = slice(k * D, (k + 1) * D)
                sp.dma_start(wqk[half, :], w_qkv[:, 0:2 * D]).then_inc(loaded, 16)
                sp.dma_start(wv[half, :], w_qkv[:, 2 * D:3 * D]).then_inc(loaded, 16)
            for k in range(2):
                half = slice(k * D, (k + 1) * D)
                sp.dma_start(wp2[half, k, :], w_proj).then_inc(loaded, 16)
                sp.dma_start(wg2[half, k, :], gate_w).then_inc(loaded, 16)
                sp.dma_start(bp2[half, :], b_proj.rearrange("(p a) -> p a", a=1)).then_inc(loaded, 16)
                sp.dma_start(bv2[half, :], b_qkv[2 * D:3 * D].rearrange("(p a) -> p a", a=1)).then_inc(loaded, 16)
            sp.dma_start(bg2[:, :], gate_b.partition_broadcast(P)).then_inc(loaded, 16)
            sp.dma_start(qk_b[:, :], b_qkv[0:2 * D].rearrange("(p a) -> p a", a=1)).then_inc(loaded, 16)

            def load_x(b, dyn=None):
                for f in range(2):
                    half = slice(f * CH, (f + 1) * CH)
                    sp.dma_start(xt[half, 0:NP, :, :].rearrange("c n t v -> c n (t v)"), xv[b, f]).then_inc(x_in, 16)
                    sp.dma_start(xt[half, NP, :, :],
                                 x[b, :, TIME - 1:TIME, :].to_broadcast([CH, TT, V])).then_inc(x_in, 16)

            def place_parts(b):
                sp.wait_ge(parts_ok, 2 * b + 2)
                parts = (qk_hi, qk_lo)
                n = P // 4
                for a in range(4):
                    rows = slice(a * n, (a + 1) * n)
                    for g in range(HG):
                        sp.dma_start(q16[rows, g, :], parts[a % 2][g * n:(g + 1) * n, R:R + L]).then_inc(q16_in, 16)
                for a in range(4):
                    rows = slice(a * n, (a + 1) * n)
                    for g in range(HG):
                        sp.dma_start(k16[rows, g, :], parts[a // 2][D + g * n:D + (g + 1) * n, :]).then_inc(k16_in, 16)

            def place_queries(b):
                need(sp, score_mm, NT * b)
                q32 = qk32[:, :, :].rearrange("p t q -> p (t q)")
                for h in range(H):
                    rows = slice(h * HD, (h + 1) * HD)
                    sp.dma_start(qd32[rows, h, :], q32[rows, R:R + L]).then_inc(q32_in, 16)

            def place_maxima(b):
                sp.wait_ge(mrow_ev, b + 1)
                for k in range(2):
                    sp.dma_start(mneg[k:k + 1, :, :], mrow[k * H:(k + 1) * H, :]).then_inc(mneg_in, 16)

            def save_h1(b):
                sp.wait_ge(h1_ok, b + 1)
                sp.dma_start(h1_all[:, bass.ds(b * TOK, TOK), :], h1[:, :, :]).then_inc(h1_saved, 16)

            load_x(0)
            sp.wait_ge(ready_p, 2)
            zsrc = qd16[:, :, :, :, :].rearrange("p g a h j -> p (g a h j)").bitcast(F32)
            rows = (E * CAP) // 5 // P
            for k in range(5):
                sp.dma_start(slots[k * rows * P:(k + 1) * rows * P, :].rearrange("(p r) d -> p (r d)", p=P),
                             zsrc[:, 0:rows * D]).then_inc(zeroed, 16)
            sp.wait_ge(zeroed, 80)
            sp.wait_ge(ready_v, 1)
            sp.wait_ge(tok_mm, 1)
            load_x(1)
            place_parts(0)
            place_queries(0)

            def body(b, first=False, last=False):
                if not first:
                    save_h1(b - 1)
                place_maxima(b)
                if not last:
                    sp.wait_ge(tok_mm, b + 2)
                    if not (isinstance(b, int) and b + 2 >= B):
                        load_x(b + 2)
                    place_parts(b + 1)
                    place_queries(b + 1)

            body(0, first=True)
            with sp.Fori(1, B - 2) as b:
                body(b)
            body(B - 2)
            body(B - 1, last=True)
            save_h1(B - 1)

            sp.wait_ge(scattered, 16 * B * TOK)
            sp.wait_ge(q32_in, 128 * B)

            def experts(pair):
                for k in range(2):
                    e = pair * 2 + k
                    need(sp, y_ev, (pair * 2 + k - 1) * NSTEP)
                    sp.dma_start(w1s[k][0:D, :], w1[e]).then_inc(w_in[k], 16)
                    sp.dma_start(w1s[k][D:D + 1, :], b1[bass.ds(e, 1), :]).then_inc(w_in[k], 16)
                    sp.dma_start(w2s[k], w2[e].rearrange("(f p) d -> p f d", p=P)).then_inc(w_in[k], 16)
                    sp.dma_start(b2s[k], b2[e].partition_broadcast(P)).then_inc(w_in[k], 16)
                    for s in range(NSTEP):
                        n = k * NSTEP + s
                        step = pair * 2 * NSTEP + n
                        need(sp, xT_mm, step - 1)
                        sp.dma_start(xin[n % 2], slots[bass.ds((e * NSTEP + s) * SL, SL), :].rearrange(
                            "(p i) d -> p i d", i=SI)).then_inc(s_in[n % 2], 16)
                        if isinstance(step, int) and step == 0:
                            continue
                        sp.wait_ge(y_ev, step)
                        m = (n + 1) % 2
                        sp.dma_start(results[bass.ds((e * NSTEP + s - 1) * SL, SL), :].rearrange(
                            "(p i) d -> p i d", i=SI), yout[m]).then_inc(y_out[m], 16)

            experts(0)
            with sp.Fori(1, E // 2) as pair:
                experts(pair)
            sp.wait_ge(y_ev, E * NSTEP)
            sp.dma_start(results[E * CAP - SL:E * CAP, :].rearrange("(p i) d -> p i d", i=SI),
                         yout[1]).then_inc(y_out[1], 16)

            def store(b, k):
                sp.wait_ge(fin_ok, b + 1)
                sp.dma_start(outv[b], fin[:, k, :, :]).then_inc(stored[k], 16)

            with sp.Fori(0, B // 2) as pair:
                for k in range(2):
                    store(pair * 2 + k, k)
            for k in range(2):
                sp.wait_ge(stored[k], 16 * B // 2)

        @block.tensor
        def _(pe):
            mm = nc.tensor.matmul

            pe.wait_ge(loaded, 16 * N_LOADS)
            for d in range(D):
                i = mm(ps[:, d * PATCH // 512, d * PATCH % 512:d * PATCH % 512 + PATCH],
                       wl[:, d, :, :].rearrange("r k c -> r (k c)"), const("dft", slice(0, 2 * F)), start=True, stop=True)
            i.then_inc(dft_mm, 1)
            pe.wait_ge(w_ready, 4)
            pe.wait_ge(ready_v, 1)
            pe.wait_ge(ready_a, 2)

            hflat = hcat[:, :, :].rearrange("p t q -> p (t q)")
            turn = nc.tensor.transpose

            def tokens(b, k):
                if k == 1:
                    pe.wait_ge(x_in, 64 * b + 64)
                    need(pe, max_rd, NC * b)
                else:
                    need(pe, h1T_ev, b - 1)
                for t in range(TT):
                    mm(ps[:, 2 + k, :], wtok[:, t, :, :].rearrange("p s d -> p (s d)"),
                       xt[:, k * 8:(k + 1) * 8, t, :], start=(t == 0), stop=(t == TT - 1))

            def tokens_padding(b):
                need(pe, vback_mm, b)
                need(pe, lgT_ev, b - 1)
                for t in range(TT):
                    i = mm(ps[D:P, 4, 0:V], wtok[:, t, 1, :], xt[:, NP, t, :], start=(t == 0), stop=(t == TT - 1))
                i.then_inc(tok_mm, 1)

            def queries_keys(b):
                pe.wait_ge(hcat_lo, b + 1)
                pe.wait_ge(hcat_hi, 2 * b + 2)
                need(pe, v_ev, 5 * b)
                for k in range(2):
                    i = mm(ps[:, 6 + k, :], wqk[:, :], hflat[:, R + 512 * k:R + 512 * (k + 1)], start=True, stop=True)
                i.then_inc(qk_mm, 1)

            def maxima(b, c):
                if c == 0:
                    pe.wait_ge(k16_in, 128 * b + 128)
                if c % (NC // QSTEPS) == 0:
                    pe.wait_ge(qd16_ok, QSTEPS * b + c // (NC // QSTEPS) + 1)
                if c >= 2:
                    pe.wait_ge(max_rd, NC * b + c - 1)
                for n in range(GC * HG):
                    g, a = GC * c + n // HG, n % HG
                    i = mm(ps[:, 2 + c % 2, n * GK:(n + 1) * GK], qd16[:, g, a, :, :].rearrange("p h j -> p (h j)"),
                           k16[:, a, g * G:g * G + GK], start=True, stop=True)
                i.then_inc(max_mm, 1)

            def maxima_rows(b):
                need(pe, exp_ok, NT * b)
                need(pe, yT_ev, b)
                for k in range(2):
                    pe.wait_ge(spread_ok, 4 * b + 2 * k + 2)
                    for n in range(2 * HG):
                        o, a = n // HG, n % HG
                        i = mm(ps[0:2 * H, k, :], sel16[:, 16 * n:16 * n + 16],
                               spread[o][:, k, a * NG // 2:(a + 1) * NG // 2, :].rearrange("p g j -> p (g j)"),
                               start=(n == 0), stop=(n == 2 * HG - 1))
                i.then_inc(mrow_mm, 1)

            def values(b):
                need(pe, centred, b)
                xeven = hcat[:, 0:TOK, :].rearrange("p (t o) q -> p o t q", o=2)
                teven = hflat[:, R:R + L].rearrange("p (t o q) -> p o t q", o=2, q=P)
                for o in range(2):
                    mm(ps[o * D:(o + 1) * D, 6, :], wv[:, :], xeven[:, o], start=True, stop=True)
                mm(ps[0:D, 4, 0:P], wv[:, :], hcat[:, TOK, :], start=True, stop=True)
                for o in range(2):
                    i = mm(ps[o * D:(o + 1) * D, 7, :], const("fold"), teven[:, o], start=True, stop=True)
                i.then_inc(vh_mm, 1)

            def values_back(b):
                pe.wait_ge(vT_ev, 3 * b + 3)
                pe.wait_ge(h_ev, b + 1)
                apart(pe)
                for t in range(TOK // 2):
                    turn(ps[:, 6, t * P:(t + 1) * P], vT[:, t, :], ident)
                turn(ps[:, 7, 0:D], vT_last[:, :], cst[0:D, COL["ident"][0]:COL["ident"][0] + D]).then_inc(vback_mm, 1)

            def scores(b, t):
                if t == 0:
                    pe.wait_ge(kwin_ok, 4 * b + 4)
                    pe.wait_ge(q32_in, 128 * b + 128)
                    pe.wait_ge(mneg_in, 32 * b + 32)
                if t >= 2:
                    pe.wait_ge(exp_ok, NT * b + t - 1)
                o = ps[:, t % 2, :]
                cols = slice(t * QT, (t + 1) * QT)
                mm(o, kwin[:, t, :], qd32[:, :, cols], start=True, stop=False)
                mm(o, ones16[:, :], mneg[:, :, cols], start=False, stop=True).then_inc(score_mm, 1)

            def weighted(b, t, front):
                if t == 0:
                    pe.wait_ge(v_ev, 5 * b + 5)
                    if front:
                        pe.wait_ge(hcat_hi, 2 * b + 4)
                if t % 4 == 0 and t:
                    pe.wait_ge(ot_ev, QUADS * b + t // 4)
                pe.wait_ge(exp_ok, NT * b + t + 1)
                for c in range(4):
                    i = mm(ps[32 * c:32 * c + 32, 4, (t % 4) * P:(t % 4 + 1) * P],
                           vals[t % 2][:, t // 2, 2 * c:2 * c + 2, :].rearrange("p h w -> p (h w)"),
                           probs[:, t % 3, 2 * c:2 * c + 2, :].rearrange("p h q -> p (h q)"), start=True, stop=True)
                i.then_inc(pv_mm, 1)

            def turn_back(b, k):
                pe.wait_ge(ot_ev, QUADS * b + k + 1)
                need(pe, norm_ok, QUADS * b + k)
                if k == 0:
                    need(pe, idx_ok, b)
                apart(pe)
                for s in range(4):
                    i = turn(ps[:, 5, s * P:(s + 1) * P], ot[:, k % 2, s, :], ident)
                i.then_inc(back_mm, 1)

            def attended_T(b):
                pe.wait_ge(norm_ok, QUADS * b + QUADS)
                pe.wait_ge(exp_ok, NT * b + NT)
                apart(pe)
                for t in range(TOK // 2):
                    i = turn(ps[:, 0, t * P:(t + 1) * P], atok[:, 2 * t:2 * t + 2, :].rearrange("p t d -> p (t d)"), ident)
                i.then_inc(aT_mm, 1)

            def projection(b):
                pe.wait_ge(aT_ev, b + 1)
                for o in range(2):
                    i = mm(ps[o * D:(o + 1) * D, 1, :], wp2[:, o, :], aT[:, :], start=True, stop=True)
                i.then_inc(proj_mm, 1)

            def rows_back(b):
                pe.wait_ge(yT_ev, b + 1)
                apart(pe)
                for t in range(TOK // 2):
                    i = turn(ps[:, 4, t * P:(t + 1) * P], yT[:, t * P:(t + 1) * P], ident)
                i.then_inc(yback_mm, 1)

            def normed_T(b):
                pe.wait_ge(h1_ok, b + 1)
                apart(pe)
                for t in range(TOK // 2):
                    i = turn(ps[:, 2, t * P:(t + 1) * P], h1[:, 2 * t:2 * t + 2, :].rearrange("p t d -> p (t d)"), ident)
                i.then_inc(h1T_mm, 1)

            def gate(b):
                pe.wait_ge(h1T_ev, b + 1)
                mm(ps[0:2 * E, 4, :], wg2[:, :, :].rearrange("p o e -> p (o e)"), h1T[:, :],
                   start=True, stop=True).then_inc(gate_mm, 1)

            def gate_back(b):
                pe.wait_ge(lgT_ev, b + 1)
                apart(pe)
                for t in range(TOK // 2):
                    i = turn(ps[:, 5, 2 * E * t:2 * E * (t + 1)], lgT[:, t * P:(t + 1) * P],
                             cst[0:2 * E, COL["ident"][0]:COL["ident"][0] + 2 * E])
                i.then_inc(gback_mm, 1)

            def counts(b):
                pe.wait_ge(oh_ok, b + 1)
                for s in range(1, TOK + 1):
                    mm(ps[:, 5, CNT + s * E:CNT + (TOK + 1) * E], ones16[:, :],
                       oh16[:, 0:TOK + 1 - s, :].rearrange("p t e -> p (t e)"),
                       start=(s == 1), stop=False, skip_group_check=True)
                mm(ps[:, 5, CNT:CNT + TOK * E], before16[:, :], oh16[:, 0:TOK, :].rearrange("p t e -> p (t e)"),
                   start=False, stop=True, skip_group_check=True).then_inc(cum_mm, 1)

            tokens(0, 1)
            tokens(0, 0)
            tokens_padding(0)
            queries_keys(0)
            for c in range(NC):
                maxima(0, c)

            def body(b, first=False, last=False):
                values(b)
                if not first:
                    normed_T(b - 1)
                maxima_rows(b)
                values_back(b)
                if not last:
                    tokens(b + 1, 1)
                if not first:
                    gate(b - 1)
                if not last:
                    tokens(b + 1, 0)
                if not first:
                    gate_back(b - 1)
                if not last:
                    tokens_padding(b + 1)
                chunks = iter(() if last else range(NC))

                def more(n):
                    for _ in range(n):
                        c = next(chunks, None)
                        if c is not None:
                            maxima(b + 1, c)

                for t in range(NT):
                    scores(b, t)
                    if t == 1 and not last:
                        queries_keys(b + 1)
                    if t == 1 and not first:
                        counts(b - 1)
                    if t:
                        weighted(b, t - 1, not last)
                    if t % 4 == 1 and t > 4:
                        turn_back(b, t // 4 - 1)
                    if t >= CHUNK_TILE:
                        more(1)
                weighted(b, NT - 1, not last)
                more(1)
                turn_back(b, QUADS - 1)
                more(2)
                attended_T(b)
                more(2)
                projection(b)
                more(2)
                rows_back(b)
                more(NC)

            body(0, first=True)
            with pe.Fori(1, B - 1) as b:
                body(b)
            body(B - 1, last=True)
            normed_T(B - 1)
            gate(B - 1)
            gate_back(B - 1)
            counts(B - 1)

            pe.wait_ge(idx_ok, B)

            def turn_slots(pair, n):
                step = pair * 2 * NSTEP + n
                uses = pair * NSTEP + n // 2
                pe.wait_ge(s_in[n % 2], 16 * uses + 16)
                need(pe, xT_ev, step - 1)
                apart(pe)
                for i in range(SI):
                    ins = nc.tensor.transpose(ps[0:D, n % 2, i * P:(i + 1) * P], xin[n % 2][:, i, :], ident)
                ins.then_inc(xT_mm, 1)

            def layer1(pair, n):
                step = pair * 2 * NSTEP + n
                k = n // NSTEP
                if n % NSTEP == 0:
                    pe.wait_ge(w_in[k], 64 * pair + 64)
                pe.wait_ge(xT_ev, step + 1)
                need(pe, hid_ev, 2 * (step - 1))
                for f in range(2):
                    i = mm(ps[:, 2 + 2 * (n % 2) + f, :], w1s[k][:, f * P:(f + 1) * P], xinT[n % 2], start=True, stop=True)
                i.then_inc(l1_mm, 1)

            def layer2(pair, n):
                step = pair * 2 * NSTEP + n
                k = n // NSTEP
                pe.wait_ge(hid_ev, 2 * step + 2)
                need(pe, y_ev, step - 1)
                for i in range(SI):
                    for f in range(2):
                        ins = mm(ps[:, 6 + n % 2, i * D:(i + 1) * D], hid[n % 2][:, f, i * P:(i + 1) * P],
                                 w2s[k][:, f, :], start=(f == 0), stop=(f == 1))
                ins.then_inc(l2_mm, 1)

            def experts(pair):
                turn_slots(pair, 0)
                for n in range(2 * NSTEP):
                    layer1(pair, n)
                    if n + 1 < 2 * NSTEP:
                        turn_slots(pair, n + 1)
                    layer2(pair, n)

            experts(0)
            with pe.Fori(1, E // 2) as pair:
                experts(pair)

        @block.scalar
        def _(act):
            act.wait_ge(loaded, 16 * N_LOADS)
            nc.scalar.activation(qk_bias[:, :], qk_b[:, :], ACT.Identity, scale=qk_scale).then_inc(ready_a, 1)
            nc.scalar.activation(sel16[:, :], const("sel"), ACT.Copy).then_inc(ready_a, 1)
            act.wait_ge(ready_a, 2)
            act.wait_ge(ready_v, 1)

            act.wait_ge(ready_v, 1)
            hflat = hcat[:, :, :].rearrange("p t q -> p (t q)")
            q32 = qk32[:, :, :].rearrange("p t q -> p (t q)")
            vflat = vT[:, :, :].rearrange("p t q -> p (t q)")

            def tokens_low(b):
                act.wait_ge(tok_mm, b + 1)
                nc.scalar.activation(hflat[0:D, R:R + L].rearrange("p (v n) -> p v n", n=NP),
                                     ps[0:D, 2:4, :].rearrange("p k (n v) -> p v (k n)", v=V),
                                     ACT.Copy).then_inc(hcat_lo, 1)

            def queries_keys(b):
                act.wait_ge(qk_mm, b + 1)
                need(act, q32_in, 128 * b)
                need(act, kwin_ok, 4 * b)
                nc.scalar.activation(q32[:, R:R + L], ps[:, 6:8, :].rearrange("p k q -> p (k q)"), ACT.Identity,
                                     bias=qk_bias[:, :], scale=qk_scale).then_inc(qk_ev, 1)

            def maxima_rows(b):
                act.wait_ge(mrow_mm, b + 1)
                need(act, mneg_in, 32 * b)
                nc.scalar.activation(mrow[:, :], ps[0:2 * H, 0:2, :].rearrange("p k q -> p (k q)"),
                                     ACT.Copy).then_inc(mrow_ev, 1)

            def values(b):
                act.wait_ge(vh_mm, b + 1)
                need(act, vback_mm, b)
                for dst, src, rows in ((vflat[0:D, R:], ps[0:D, 6, R:], slice(0, D)), (vflat[D:P, :], ps[D:P, 6, :], slice(D, P)),
                                       (vT_last[:, 0:R], ps[0:D, 4, 0:R], slice(0, D))):
                    nc.scalar.activation(dst, src, ACT.Identity, bias=bv2[rows, :]).then_inc(vT_ev, 1)
                need(act, yT_ev, b)
                nc.scalar.activation(hT[:, :], ps[:, 7, :], ACT.Copy).then_inc(h_ev, 1)

            def normed_T(b):
                act.wait_ge(h1T_mm, b + 1)
                need(act, gate_mm, b)
                nc.scalar.activation(h1T[:, :], ps[:, 2, :], ACT.Copy).then_inc(h1T_ev, 1)

            def logits_T(b):
                act.wait_ge(gate_mm, b + 1)
                need(act, gback_mm, b)
                nc.scalar.activation(lgT[:, :], ps[0:2 * E, 4, :], ACT.Copy).then_inc(lgT_ev, 1)

            def gate_weights(b):
                act.wait_ge(gate_sub, b + 1)
                nc.scalar.activation(ex[:, :, :], lg[:, :, :], ACT.Exp).then_inc(gate_exp, 1)

            def sums_out(b, k):
                act.wait_ge(pv_mm, NT * b + 4 * k + 4)
                need(act, back_mm, QUADS * b + k - 1)
                nc.scalar.activation(ot[:, k % 2, :, :].rearrange("p s c -> p (s c)"), ps[:, 4, :],
                                     ACT.Copy).then_inc(ot_ev, 1)

            tokens_low(0)
            queries_keys(0)

            def body(b, first=False, last=False):
                values(b)
                if not first:
                    normed_T(b - 1)
                maxima_rows(b)
                if not first:
                    logits_T(b - 1)
                if not last:
                    tokens_low(b + 1)
                for t in range(NT):
                    act.wait_ge(score_mm, NT * b + t + 1)
                    need(act, pv_mm, NT * b + t - 2)
                    nc.scalar.activation(probs[:, t % 3, :, :].rearrange("p h q -> p (h q)"), ps[:, t % 2, :],
                                         ACT.Exp).then_inc(exp_ok, 1)
                    if t == 0 and not first:
                        gate_weights(b - 1)
                    if t == 1 and not last:
                        queries_keys(b + 1)
                    if t % 4 == 0 and t:
                        sums_out(b, t // 4 - 1)
                sums_out(b, QUADS - 1)
                act.wait_ge(aT_mm, b + 1)
                need(act, proj_mm, b)
                nc.scalar.activation(aT[:, :], ps[:, 0, :], ACT.Copy).then_inc(aT_ev, 1)

            body(0, first=True)
            with act.Fori(1, B - 1) as b:
                body(b)
            body(B - 1, last=True)
            normed_T(B - 1)
            logits_T(B - 1)
            gate_weights(B - 1)

            def experts(pair):
                for n in range(2 * NSTEP):
                    step = pair * 2 * NSTEP + n
                    act.wait_ge(l1_mm, step + 1)
                    need(act, l2_mm, step - 1)
                    nc.scalar.activation(hid[n % 2][:, 0, :], ps[:, 2 + 2 * (n % 2), :], ACT.Relu).then_inc(hid_ev, 1)

            experts(0)
            with act.Fori(1, E // 2) as pair:
                experts(pair)

        @block.gpsimd
        def _(pool):
            nc.gpsimd.memset(qd16[:, :, :, :, :].rearrange("p g a h j -> p (g a h j)"), 0.0).then_inc(ready_p, 1)
            nc.gpsimd.memset(mneg[:, :, :].rearrange("p h q -> p (h q)"), 0.0).then_inc(ready_p, 1)
            pool.wait_ge(ready_v, 1)
            pool.wait_ge(loaded, 16 * N_LOADS)

            def diagonal(b):
                pool.wait_ge(q16_in, 128 * b + 128)
                need(pool, max_mm, NC * b)
                n = NG // QSTEPS
                for k in range(QSTEPS):
                    for a in range(HG):
                        src = q16[:, a, k * n * G:(k + 1) * n * G].rearrange("p (g j) -> p g j", j=G)
                        i = nc.gpsimd.tensor_tensor(
                            qd16[:, k * n:(k + 1) * n, a, :, :], src.unsqueeze(2).to_broadcast([P, n, HW, G]),
                            const("heads").unsqueeze(1).unsqueeze(3).to_broadcast([P, n, HW, G]), ALU.mult)
                    i.then_inc(qd16_ok, 1)

            def spread_maxima(b, k):
                need(pool, mrow_mm, b)
                n = HG * NG // 2
                for o, part in enumerate((mx_hi, mx_lo)):
                    pool.wait_ge(mx_ok, 4 * b + 2 * k + 1 + o)
                    nc.gpsimd.tensor_tensor(
                        spread[o][:, k, :, :],
                        part[:, k, :, :].rearrange("p a g -> p (a g)").unsqueeze(2).to_broadcast([P, n, G]),
                        const("delta").unsqueeze(1).to_broadcast([P, n, G]), ALU.mult).then_inc(spread_ok, 1)

            def inv_std(src, dst, ready, done, n):
                pool.wait_ge(ready, n)
                nc.gpsimd.tensor_tensor(dst, src, minus_half.to_broadcast([P, TOK]), ALU.pow).then_inc(done, 1)

            def scatter(b):
                pool.wait_ge(idx_ok, b + 1)
                apart(pool)
                for t in range(TOK):
                    nc.gpsimd.indirect_dma_start(
                        out=slots, out_offset=bass.IndirectOffsetOnAxis(ap=sidx[:, t:t + 1], axis=0),
                        in_=h1[:, t, :], in_offset=None).then_inc(scattered, 16)

            pool.wait_ge(zeroed, 80)
            diagonal(0)
            for k in range(2):
                spread_maxima(0, k)

            def body(b, first=False, last=False):
                if not first:
                    scatter(b - 1)
                if not last:
                    diagonal(b + 1)
                    spread_maxima(b + 1, 0)
                inv_std(st[:, 1, :], st[:, 2, :], var_ok, rstd_ok, b + 1)
                if not last:
                    spread_maxima(b + 1, 1)

            body(0, first=True)
            with pool.Fori(1, B - 1) as b:
                body(b)
            body(B - 1, last=True)
            scatter(B - 1)

            for m in range(2):
                pool.wait_ge(y_out[m], 16 * E * NSTEP // 2)

            def gather(pair):
                for k in range(2):
                    b = pair * 2 + k
                    pool.wait_ge(gidx_ok, b + 1)
                    need(pool, fin_ok, b - 1)
                    apart(pool)
                    for t in range(TOK):
                        nc.gpsimd.indirect_dma_start(
                            out=yg[:, k, t, :], out_offset=None, in_=results,
                            in_offset=bass.IndirectOffsetOnAxis(ap=gidx[:, k, t:t + 1], axis=0)).then_inc(gathered[k], 16)
                    if isinstance(b, int) and b == 0:
                        continue
                    inv_std(st[:, 1, :], st[:, 2, :], fvar_ok, frstd_ok, b)

            gather(0)
            with pool.Fori(1, B // 2) as pair:
                gather(pair)
            inv_std(st[:, 1, :], st[:, 2, :], fvar_ok, frstd_ok, B)

        @block.vector
        def _(dve):
            own = Chain(dve, dve_own)
            link = own.link
            v = nc.vector
            dve.wait_ge(loaded, 16 * N_LOADS)
            dve.wait_ge(ready_p, 2)

            link(v.memset(place[0:D, :], 0.0))
            link(v.tensor_copy(place[D:P, :].rearrange("p (n j) -> p n j", j=QT),
                               const("onehot", slice(D, P)).unsqueeze(1).to_broadcast([D, H * L // QT, QT])))
            for o in range(2):
                link(v.tensor_copy(kwin[D:P, :, :].rearrange("p (t o) k -> p o t k", o=2)[:, o],
                                   cst[D:P, COL["keymask"][0] + o * P:COL["keymask"][0] + (o + 1) * P]
                                   .unsqueeze(1).to_broadcast([D, NT // 2, P])))
                link(v.memset(vals[o][:, :, :, :].rearrange("p t h w -> p (t h w)"), 0.0))
                link(v.memset(vals[o][:, :, :, HD:HD + 1], 1.0))
            link(v.memset(hcat[:, :, :].rearrange("p t q -> p (t q)"), 0.0))
            link(v.memset(qk32[:, :, :].rearrange("p t q -> p (t q)"), 0.0))
            link(v.memset(vT[0:D, 0, 0:R], 0.0))
            link(v.memset(vT_last[:, :], 0.0))
            for w in (wp2, wg2):
                for k in range(2):
                    link(v.memset(w[k * D:(k + 1) * D, 1 - k, :], 0.0))
            link(v.memset(ones16[:, :], 1.0))
            link(v.tensor_copy(before16[:, :], const("before")))
            link(v.memset(oh16[:, :, :].rearrange("p t e -> p (t e)"), 0.0))
            link(v.memset(run[:, :], 0.0))
            v.nop().then_inc(ready_v, 1)
            dve.wait_ge(dft_mm, 1)
            wps = ps[:, 0:2, :].rearrange("p k (d t) -> p (k d) t", t=PATCH)
            for f in range(2):
                half = slice(f * CH, (f + 1) * CH)
                for s in range(2):
                    t0 = s * STRIDE + f * TT
                    v.tensor_copy(wtok[half, :, s, :], wps[half, :, t0:t0 + TT].rearrange("p d t -> p t d")
                                  ).then_inc(w_ready, 1)

            hflat = hcat[:, :, :].rearrange("p t q -> p (t q)")
            q32 = qk32[:, :, :].rearrange("p t q -> p (t q)")

            def tokens_high(b):
                dve.wait_ge(tok_mm, b + 1)
                hv = hflat[D:P, R:R + L].rearrange("p (v n) -> p v n", n=NP)
                v.tensor_copy(hv[:, :, 0:NP - 1],
                              ps[D:P, 2:4, :].rearrange("p k (n v) -> p v (k n)", v=V)[:, :, 1:NP]).then_inc(hcat_hi, 1)
                v.tensor_copy(hv[:, :, NP - 1:NP], ps[D:P, 4, 0:V].unsqueeze(2)).then_inc(hcat_hi, 1)

            def parts(b):
                dve.wait_ge(qk_ev, b + 1)
                need(dve, q16_in, 128 * b)
                need(dve, k16_in, 128 * b)
                v.tensor_copy(qk_hi[:, :], q32[:, 0:XP]).then_inc(parts_ok, 1)
                dve.wait_ge(parts_ok, 2 * b + 1)
                v.tensor_tensor(qk_lo[:, :], q32[:, 0:XP], qk_hi[:, :], ALU.subtract).then_inc(parts_ok, 1)

            def windows(b):
                dve.wait_ge(qk_ev, b + 1)
                need(dve, score_mm, NT * b)
                kw = kwin[0:D, :, :].rearrange("p (t o) (f k) -> p o f t k", o=2, f=2)
                for o, f, t0, f0 in ((0, 0, 0, 0), (0, 1, 0, 1), (1, 1, 0, 1), (1, 0, 1, 0)):
                    v.tensor_copy(kw[:, o, f], qk32[D:P, t0:t0 + TOK, f0 * QT:(f0 + 1) * QT]).then_inc(kwin_ok, 1)

            def maxima(b, c):
                need(dve, max_rd, NC * b + c - 1)
                dve.wait_ge(max_mm, NC * b + c + 1)
                apart(dve)
                for n in range(GC * HG):
                    g, a = GC * c + n // HG, n % HG
                    k, g = divmod(g, NG // 2)
                    i = v.tensor_tensor_reduce(junk[:, c % 2 * GC * HG + n, :], ps[:, 2 + c % 2, n * GK:(n + 1) * GK],
                                               const("winmask"), 1.0, -3e38, ALU.add, ALU.max, mx[:, k, a, g:g + 1])
                i.then_inc(max_rd, 1)

            def maxima_parts(b, k):
                dve.wait_ge(max_rd, NC * b + (k + 1) * NC // 2)
                need(dve, spread_ok, 4 * b)
                v.tensor_scalar(mx_hi[:, k], mx[:, k], -1.0, None, ALU.mult).then_inc(mx_ok, 1)
                dve.wait_ge(mx_ok, 4 * b + 2 * k + 1)
                link(v.tensor_tensor(mx_rest[:, k], mx[:, k], mx_hi[:, k], ALU.add))
                v.tensor_scalar(mx_lo[:, k], mx_rest[:, k], -1.0, None, ALU.mult).then_inc(mx_ok, 1)

            def values(b):
                dve.wait_ge(vback_mm, b + 1)
                pv = ps[:, 6, :].rearrange("p (t h d) -> p t h d", h=H, d=HD)
                p9 = ps[:, 7, 0:D].rearrange("p (t h d) -> p t h d", t=1, d=HD)
                e, o = (u[:, :, :, 0:HD] for u in vals)
                v.tensor_copy(e, pv).then_inc(v_ev, 1)
                v.tensor_copy(o[D:P], pv[D:P]).then_inc(v_ev, 1)
                v.tensor_copy(o[0:D, 0:TOK - 1], pv[0:D, 1:TOK]).then_inc(v_ev, 1)
                v.tensor_copy(o[0:D, TOK - 1:TOK], p9[0:D]).then_inc(v_ev, 2)

            def normalize(b, k):
                dve.wait_ge(back_mm, QUADS * b + k + 1)
                bank = ps[:, 5, :].rearrange("p (s c h w) -> p s c h w", s=4, c=4, h=2)
                for hh in range(2):
                    half = slice(hh * D, (hh + 1) * D)
                    i = v.reciprocal(rden[half, k % 2, :, :], bank[half, :, :, hh, HD])
                link(i)
                at = atok[:, :, :].rearrange("p t (c h d) -> p t c h d", c=4, h=2)
                for hh in range(2):
                    half = slice(hh * D, (hh + 1) * D)
                    for s in range(4):
                        i = v.tensor_tensor(
                            at[(s % 2) * D:(s % 2 + 1) * D, 2 * k + s // 2, :, hh, :], bank[half, s, :, hh, 0:HD],
                            rden[half, k % 2, s, :].unsqueeze(2).to_broadcast([D, 4, HD]), ALU.mult)
                i.then_inc(norm_ok, 1)

            def bc(a, n):
                return a.unsqueeze(2).to_broadcast([P, TOK, n])

            def norm_stats(src, ready, read=None):
                link(v.tensor_reduce(st[:, 0, :], src, AX, ALU.add))
                link(v.tensor_scalar(st[:, 3, :], st[:, 0, :], 1.0 / D, None, ALU.mult))
                i = v.tensor_tensor(yc[:, :, :], src, bc(st[:, 3, :], D), ALU.subtract)
                if read is None:
                    link(i)
                else:
                    i.then_inc(read[0], 1)
                    dve.wait_ge(*read)
                link(v.tensor_tensor(sq[:, :, :], yc[:, :, :], yc[:, :, :], ALU.mult))
                link(v.tensor_reduce(st[:, 4, :], sq[:, :, :], AX, ALU.add))
                v.tensor_scalar(st[:, 1, :], st[:, 4, :], 1.0 / D, EPS, ALU.mult, ALU.add).then_inc(ready, 1)

            def residual(b):
                dve.wait_ge(proj_mm, b + 1)
                dve.wait_ge(h_ev, b + 1)
                need(dve, yback_mm, b)
                v.scalar_tensor_tensor(out=yT[:, :], in0=ps[:, 1, :], scalar=bp2[:, :], in1=hT[:, :],
                                       op0=ALU.add, op1=ALU.add).then_inc(yT_ev, 1)

            def first_stats(b):
                dve.wait_ge(yback_mm, b + 1)
                norm_stats(ps[:, 4, :].rearrange("p (t d) -> p t d", d=D), var_ok, (centred, b + 1))

            def first_norm(b):
                dve.wait_ge(rstd_ok, b + 1)
                need(dve, scattered, 16 * TOK * b)
                need(dve, h1_saved, 16 * b)
                need(dve, h1T_mm, b)
                v.tensor_tensor(h1[:, :, :], yc[:, :, :], bc(st[:, 2, :], D), ALU.mult).then_inc(h1_ok, 1)

            lmax, esum, prb, code, pos, ebase, kept, t0, t1, t2 = (rt[:, k, :] for k in range(10))

            def route(b):
                dve.wait_ge(gback_mm, b + 1)
                link(v.tensor_tensor(logit[:, :, :], ps[:, 5, 0:TOK * E].rearrange("p (t e) -> p t e", e=E),
                                     bg2[:, :].unsqueeze(1).to_broadcast([P, TOK, E]), ALU.add))
                link(v.tensor_reduce(lmax, logit[:, :, :], AX, ALU.max))
                v.tensor_tensor(lg[:, :, :], logit[:, :, :], bc(lmax, E), ALU.subtract).then_inc(gate_sub, 1)
                dve.wait_ge(gate_sub, b + 1)
                link(v.tensor_scalar(cand[:, :, :], lg[:, :, :], 0.0, None, ALU.is_ge))
                link(v.tensor_tensor(cand[:, :, :], cand[:, :, :],
                                     const("rev").unsqueeze(1).to_broadcast([P, TOK, E]), ALU.mult))
                link(v.tensor_reduce(code, cand[:, :, :], AX, ALU.max))
                v.tensor_tensor(oh16[:, 0:TOK, :], cand[:, :, :], bc(code, E), ALU.is_equal).then_inc(oh_ok, 1)

            def slots_of(b):
                dve.wait_ge(gate_exp, b + 1)
                link(v.tensor_reduce(esum, ex[:, :, :], AX, ALU.add))
                link(v.reciprocal(prb, esum))
                dve.wait_ge(oh_ok, b + 1)
                dve.wait_ge(cum_mm, b + 1)
                cnt = ps[:, 5, CNT:CNT + (TOK + 1) * E].rearrange("p (t e) -> p t e", e=E)
                link(v.tensor_tensor(posw[:, :, :], cnt[:, 0:TOK, :],
                                     run[:, :].unsqueeze(1).to_broadcast([P, TOK, E]), ALU.add))
                link(v.tensor_tensor(posw[:, :, :], posw[:, :, :], oh16[:, 0:TOK, :], ALU.mult))
                link(v.tensor_reduce(pos, posw[:, :, :], AX, ALU.add))
                link(v.tensor_tensor(run[:, :], cnt[:, TOK, :], run[:, :], ALU.add))
                link(v.tensor_scalar(ebase, code, float(-CAP), float(E * CAP), ALU.mult, ALU.add))
                link(v.tensor_scalar(kept, pos, float(CAP), None, ALU.is_lt))
                link(v.tensor_tensor(t0, ebase, pos, ALU.add))
                link(v.tensor_tensor(t0, t0, const("trash"), ALU.subtract))
                link(v.tensor_tensor(t0, t0, kept, ALU.mult))
                need(dve, scattered, 16 * TOK * b)
                v.tensor_tensor(sidx[:, :], t0, const("trash"), ALU.add).then_inc(idx_ok, 1)
                link(v.tensor_scalar(t1, pos, float(CAP - 1), None, ALU.min))
                cols = bass.ds(b * TOK, TOK)
                link(v.tensor_tensor(gidx_all[:, cols], t1, ebase, ALU.add))
                link(v.tensor_tensor(w_all[:, cols], prb, kept, ALU.mult))

            tokens_high(0)
            parts(0)
            windows(0)
            for c in range(NC):
                maxima(0, c)
            for k in range(2):
                maxima_parts(0, k)

            def body(b, first=False, last=False):
                values(b)
                if not last:
                    tokens_high(b + 1)
                if not first:
                    route(b - 1)
                    slots_of(b - 1)
                if not last:
                    parts(b + 1)
                chunks = iter(() if last else range(NC))

                def more(n):
                    for _ in range(n):
                        c = next(chunks, None)
                        if c is not None:
                            maxima(b + 1, c)
                            if c == NC // 2 - 1:
                                maxima_parts(b + 1, 0)

                for k in range(QUADS - 1):
                    done = max(0, 4 * k + 5 - CHUNK_TILE)
                    before = max(0, 4 * k + 1 - CHUNK_TILE)
                    more(done - before)
                    normalize(b, k)
                more(NT - max(CHUNK_TILE, 4 * QUADS - 3) + 1)
                normalize(b, QUADS - 1)
                if not last:
                    windows(b + 1)
                more(4)
                residual(b)
                more(2)
                first_stats(b)
                more(NC)
                if not last:
                    maxima_parts(b + 1, 1)
                first_norm(b)

            body(0, first=True)
            peeled = own.n
            with dve.Fori(1, B - 1) as b:
                own.rebase(peeled + (b - 1) * LINKS)
                body(b)
                assert own.n == LINKS, own.n
            own.rebase(peeled + (B - 2) * LINKS)
            body(B - 1, last=True)
            route(B - 1)
            slots_of(B - 1)

            for k in range(2):
                link(v.memset(xinT[k][D:D + 1, :], 1.0))

            def turned(pair, n):
                step = pair * 2 * NSTEP + n
                dve.wait_ge(xT_mm, step + 1)
                need(dve, l1_mm, step - 1)
                v.tensor_copy(xinT[n % 2][0:D, :], ps[0:D, n % 2, :]).then_inc(xT_ev, 1)

            def experts(pair):
                turned(pair, 0)
                for n in range(2 * NSTEP):
                    step = pair * 2 * NSTEP + n
                    dve.wait_ge(l1_mm, step + 1)
                    need(dve, l2_mm, step - 1)
                    v.tensor_scalar(hid[n % 2][:, 1, :], ps[:, 3 + 2 * (n % 2), :], 0.0, None, ALU.max).then_inc(hid_ev, 1)
                    if n + 1 < 2 * NSTEP:
                        turned(pair, n + 1)
                    dve.wait_ge(l2_mm, step + 1)
                    need(dve, y_out[n % 2], 16 * (pair * NSTEP + n // 2))
                    v.tensor_tensor(yout[n % 2], ps[:, 6 + n % 2, 0:SI * D].rearrange("p (i d) -> p i d", i=SI),
                                    b2s[n // NSTEP].unsqueeze(1).to_broadcast([P, SI, D]), ALU.add).then_inc(y_ev, 1)

            experts(0)
            with dve.Fori(1, E // 2) as pair:
                experts(pair)

            dve.wait_ge(h1_saved, 16 * B)

            def indices(b, k):
                v.tensor_copy(gidx[:, k, :], gidx_all[:, bass.ds(b * TOK, TOK)]).then_inc(gidx_ok, 1)

            def finish(pair, k):
                b = pair * 2 + k
                dve.wait_ge(gathered[k], 16 * TOK * (pair + 1))
                g = yg[:, k, :, :]
                cols = bass.ds(b * TOK, TOK)
                link(v.tensor_tensor(g, g, bc(w_all[:, cols], D), ALU.mult))
                link(v.tensor_scalar(bad[:, :, :], g, 0.0, 0.0, ALU.mult, ALU.not_equal))
                link(v.tensor_scalar(sq[:, :, :], g, -1e4, 1e4, ALU.max, ALU.min))
                link(v.tensor_tensor(y[:, :, :], g, g, ALU.is_equal))
                link(v.tensor_tensor(sq[:, :, :], sq[:, :, :], y[:, :, :], ALU.mult))
                apart(dve)
                link(v.copy_predicated(g, bad[:, :, :], sq[:, :, :]))
                link(v.tensor_tensor(y[:, :, :], g, h1_all[:, cols, :], ALU.add))
                norm_stats(y[:, :, :], fvar_ok)
                dve.wait_ge(frstd_ok, b + 1)
                need(dve, stored[k], 16 * pair)
                v.tensor_tensor(fin[:, k, :, :], yc[:, :, :], bc(st[:, 2, :], D), ALU.mult).then_inc(fin_ok, 1)

            indices(0, 0)
            indices(1, 1)

            def finish_pair(pair, more):
                for k in range(2):
                    finish(pair, k)
                    if more:
                        indices(pair * 2 + k + 2, k)

            start = own.n
            base = own.base
            finish_pair(0, True)
            per_pair = own.n - start
            with dve.Fori(1, B // 2 - 1) as pair:
                own.rebase(base + start + pair * per_pair)
                finish_pair(pair, True)
            own.rebase(base + start + (B // 2 - 1) * per_pair)
            finish_pair(B // 2 - 1, False)


_INS = ["x", "L0_tok_W", "L0_attn_w_qkv", "L0_attn_b_qkv", "L0_attn_w_proj", "L0_attn_b_proj", "L0_ffn_gate_w",
        "L0_ffn_gate_b", "L0_ffn_w1", "L0_ffn_b1", "L0_ffn_w2", "L0_ffn_b2"]


def kernel(**inputs):
    import concourse.bacc as _bacc
    from concourse.bass_utils import run_bass_kernel_spmd as _run

    nc = _bacc.Bacc("TRN2", target_bir_lowering=False, num_devices=1)
    arrays, args = {}, []
    for name in _INS:
        a = np.ascontiguousarray(inputs[name])
        arrays[f"in_{name}"] = a
        args.append(nc.dram_tensor(f"in_{name}", a.shape, mybir.dt.from_np(a.dtype), kind="ExternalInput").ap())
    arrays["in_consts"] = constants()
    args.append(nc.dram_tensor("in_consts", (P, NCONST), F32, kind="ExternalInput").ap())
    args.append(nc.dram_tensor("out_0", (B, L, D), F32, kind="ExternalOutput").ap())
    build(nc, *args)
    r = _run(nc, [arrays], core_ids=[0])
    return r.results[0]["out_0"]
```

```python
from contextlib import ExitStack

import numpy as np

import concourse.bass as bass
from concourse import mybir

ALU = mybir.AluOpType
ACT = mybir.ActivationFunctionType
AX = mybir.AxisListType.X
F32 = mybir.dt.float32
BF16 = mybir.dt.bfloat16
I32 = mybir.dt.int32

P = 128
B, CH, TIME, V = 16, 64, 128, 64
PATCH, STRIDE = 16, 8
NP = TIME // STRIDE
L = V * NP
D = 64
F = PATCH // 2 + 1
NBLK = NP + 1
TT = STRIDE // 2
H, HD, R = 8, 8, 32
QT = 64
NT = L // QT
XP = L + 2 * R
G = 32
NG = L // G
GK = G + 2 * R
HG, HW = 2, 4
GC = 2
NC = NG // GC
QSTEPS = 2
TOK = L // P
E, FF = 8, 256
CAP = -(-5 * B * L // (4 * E))
SL = 512
NSTEP = CAP // SL
SI = SL // P
SE = CAP // P
RW = D + 2
NOBODY = 1 << 20
EPS = 1e-5
LINKS = 31
LINKS_B = 112
BIG = 1e30
VW = 16
CNT = TOK * E
AFTER_TILE = [0] * 9 + [1, 1, 2, 2, 2, 2, 2]
DIAGONAL_TILES = [6, 7, 9, 10]
TOKENS_LAST = [0, 2, 1, 1, 2]
AFTER_LAST = [1, 2, 1, 0, NC]
QUADS = NT // 4

_widths = dict(ident=P, fold=D, keymask=2 * P, onehot=QT, winmask=GK, delta=G, before=P, sel=4 * 16,
               dft=PATCH, rev=E, unit=2, trash=TOK, number=TOK, heads=HW)
COL, _at = {}, 0
for _n, _w in _widths.items():
    COL[_n] = (_at, _at + _w)
    _at += _w
NCONST = _at


def constants():
    c = np.zeros((P, NCONST), np.float32)

    def put(name, a, rows=slice(0, P)):
        c[rows, COL[name][0]:COL[name][0] + a.shape[1]] = a

    p = np.arange(P)
    put("ident", np.eye(P))
    put("fold", np.concatenate([np.eye(D)] * 2))
    key, j = np.arange(P)[None], np.arange(QT)[:, None]
    for odd in range(2):
        at = key if not odd else (key + QT) % P
        c[QT:, COL["keymask"][0] + odd * P:COL["keymask"][0] + (odd + 1) * P] = np.where(
            (at < j) | (at > j + 2 * R), -BIG, 0)
    put("onehot", np.eye(QT), slice(QT, P))
    kk, jj = np.arange(GK)[None], (p % G)[:, None]
    put("winmask", np.where((kk < jj) | (kk > jj + 2 * R), -BIG, 0))
    put("delta", (p % G)[:, None] == np.arange(G)[None])
    put("before", p[:, None] < p[None])
    put("sel", np.concatenate([(p // G)[:, None] + H * o + HW * g == np.arange(16)[None]
                               for o in range(2) for g in range(HG)], 1))
    f, t = np.arange(F)[:, None], np.arange(PATCH)[None]
    angle = 2 * np.pi * ((f * t) % PATCH) / PATCH
    put("dft", np.concatenate([np.cos(angle), -np.sin(angle)]) / np.sqrt(PATCH), slice(0, 2 * F))
    put("heads", ((p % (P // 4)) // HD)[:, None] == np.arange(HW)[None])
    put("number", np.arange(TOK)[None] * P + p[:, None])
    put("rev", np.broadcast_to(E - np.arange(E), (P, E)))
    put("unit", np.stack([np.where(p < D, HD ** -0.5, 1), 0 * p - 0.5], 1))
    put("trash", E * CAP + np.arange(TOK)[None] * P + p[:, None])
    return c


class Chain:

    def __init__(self, eng, sem):
        self.eng, self.sem, self.base, self.n = eng, sem, 0, 0

    def put(self, ins):
        self.n += 1
        ins.then_inc(self.sem, 1)
        return self.base + self.n

    def after(self, count):
        self.eng.wait_ge(self.sem, count)

    def link(self, ins):
        self.after(self.put(ins))

    def rebase(self, base):
        self.base, self.n = base, 0


def need(eng, sem, value):
    if not isinstance(value, int) or value > 0:
        eng.wait_ge(sem, value)


def build(nc, x, w_tok, w_qkv, b_qkv, w_proj, b_proj, gate_w, gate_b, w1, b1, w2, b2, consts, out):
    with ExitStack() as ctx:
        def sb(name, shape, dt=F32):
            return ctx.enter_context(nc.sbuf_tensor(name, shape, dt))

        def sem(name):
            return ctx.enter_context(nc.semaphore(name))

        slots = nc.dram_tensor("slots", [E * CAP + TOK * P, RW], F32).ap()

        cst = sb("cst", [P, NCONST])

        def const(name, rows=slice(0, P)):
            return cst[rows, COL[name][0]:COL[name][1]]

        ident = const("ident")
        before16 = sb("before16", [P, P], BF16)
        ones16 = sb("ones16", [P, P], BF16)
        sel16 = sb("sel16", [P, 64], BF16)
        wtok = sb("wtok", [P, TT, 2, D])
        wqk = sb("wqk", [P, 2 * D])
        wv = sb("wv", [P, D])
        wp2 = sb("wp2", [P, 2, D])
        bp2 = sb("bp2", [P, 1])
        bv2 = sb("bv2", [P, 1])
        wg2 = sb("wg2", [P, 2, E])
        bg2 = sb("bg2", [P, E])
        qk_scale = cst[:, COL["unit"][0]:COL["unit"][0] + 1]
        minus_half = cst[:, COL["unit"][0] + 1:COL["unit"][0] + 2]
        qk_b = sb("qk_b", [P, 1])
        qk_bias = sb("qk_bias", [P, 1])
        xt = sb("xt", [P, NBLK, TT, V])
        hcat = sb("hcat", [P, TOK + 1, P])
        qk32 = sb("qk32", [P, TOK + 1, P])
        qk_hi = sb("qk_hi", [P, XP], BF16)
        qk_lo = sb("qk_lo", [P, XP], BF16)
        q16 = sb("q16", [P, HG, L], BF16)
        k16 = sb("k16", [P, HG, XP], BF16)
        qd16 = sb("qd16", [P, NG, HG, HW, G], BF16)
        qd32 = sb("qd32", [P, H, L])
        kwin = sb("kwin", [P, NT, P])
        mneg = sb("mneg", [P, H, L], BF16)
        vals = [sb(f"vals{o}", [P, TOK, H, VW]) for o in range(2)]
        vT = sb("vT", [P, TOK // 2, P])
        vT_last = sb("vT_last", [D, P])
        hT = sb("hT", [P, TOK // 2 * P])
        junk = sb("junk", [P, 2 * GC * HG, GK])
        mx = sb("mx", [P, 2, HG, NG // 2])
        mx_hi = sb("mx_hi", [P, 2, HG, NG // 2], BF16)
        mx_rest = sb("mx_rest", [P, 2, HG, NG // 2])
        mx_lo = sb("mx_lo", [P, 2, HG, NG // 2], BF16)
        spread = [sb(f"spread{o}", [P, 2, HG * NG // 2, G], BF16) for o in range(2)]
        mrow = sb("mrow", [2 * H, L], BF16)
        probs = sb("probs", [P, 3, H, QT])
        ot = sb("ot", [P, 2, 4, P])
        rden = sb("rden", [P, 2, 4, 4])
        atok = sb("atok", [P, TOK, D])
        aT = sb("aT", [P, L // 2])
        yT = sb("yT", [P, L // 2])
        y = sb("y", [P, TOK, D])
        yc = sb("yc", [P, TOK, D])
        sq = sb("sq", [P, TOK, D])
        st = sb("st", [P, 8, TOK])
        h1 = sb("h1", [P, TOK, D])
        h1x = sb("h1x", [P, TOK, RW])
        out2 = sb("out2", [P, TOK, D])
        h1T = sb("h1T", [P, L // 2])
        lgT = sb("lgT", [2 * E, L // 2])
        wl = mneg[0:2 * F, :, :].rearrange("p h q -> p (h q)").bitcast(F32).rearrange(
            "p (d c) -> p d c", c=CH)
        logit = sb("logit", [P, TOK, E])
        lg = sb("lg", [P, TOK, E])
        ex = sb("ex", [P, TOK, E])
        cand = sb("cand", [P, TOK, E])
        oh16 = sb("oh16", [P, TOK + 1, E], BF16)
        posw = sb("posw", [P, TOK, E])
        rt = sb("rt", [P, 16, TOK])
        run = sb("run", [P, E])
        number = sb("number", [P, TOK])
        sidx = sb("sidx", [P, TOK], I32)
        fill = qd16[:, :, :, :, :].rearrange("p g a h j -> p (g a h j)").bitcast(F32)[:, 0:32 * RW].rearrange(
            "p (r c) -> p r c", c=RW)

        place = qd32[:, :, :].rearrange("p h q -> p (h q)")
        taken = [0]

        def again(width, rows=P):
            a = taken[0]
            taken[0] += width
            assert taken[0] <= H * L
            return place[0:rows, a:a + width]

        w1s = [again(FF) for _ in range(2)]
        w2s = [again(2 * D).rearrange("p (f d) -> p f d", f=2) for _ in range(2)]
        b2s = [again(1) for _ in range(2)]
        xinT = [again(SL) for _ in range(2)]
        hid = [again(2 * SL).rearrange("p (f s) -> p f s", f=2) for _ in range(2)]
        resT = again(SL // 2)
        fin = [again(SI * D).rearrange("p (i d) -> p i d", i=SI) for _ in range(2)]
        res, subst, same, total, square = (again(SI * D).rearrange("p (i d) -> p i d", i=SI) for _ in range(5))
        cent = [again(SI * D).rearrange("p (i d) -> p i d", i=SI) for _ in range(2)]
        bad = again(SI * D).rearrange("p (i d) -> p i d", i=SI).bitcast(I32)
        fst = again(8 * SI).rearrange("p (k i) -> p k i", i=SI)
        ids = [again(SE).bitcast(I32) for _ in range(2)]
        xin = [sb(f"xin{k}", [P, SE, RW]) for k in range(2)]

        ps = ctx.enter_context(nc.psum_tensor("ps", [P, 8, 512], F32))

        tables_in, loaded = sem("tables_in"), sem("loaded")
        dft_mm, w_ready, ready_v, ready_p, ready_a = (sem(n) for n in ("dft_mm", "w_ready", "ready_v", "ready_p", "ready_a"))
        zeroed = sem("zeroed")
        x_in, tok_mm, hcat_lo, hcat_hi = (sem(n) for n in ("x_in", "tok_mm", "hcat_lo", "hcat_hi"))
        qk_mm, qk_ev, parts_ok, kwin_ok = (sem(n) for n in ("qk_mm", "qk_ev", "parts_ok", "kwin_ok"))
        q16_in, k16_in, qd16_ok, qd16_last, q32_in, mneg_in = (
            sem(n) for n in ("q16_in", "k16_in", "qd16_ok", "qd16_last", "q32_in", "mneg_in"))
        max_mm, max_rd, mx_ok, spread_ok, mrow_mm, mrow_ev = (
            sem(n) for n in ("max_mm", "max_rd", "mx_ok", "spread_ok", "mrow_mm", "mrow_ev"))
        vh_mm, vT_ev, h_ev, vback_mm, v_ev = (sem(n) for n in ("vh_mm", "vT_ev", "h_ev", "vback_mm", "v_ev"))
        yT_ev, yback_mm, centred, lgT_ev, gback_mm = (sem(n) for n in ("yT_ev", "yback_mm", "centred", "lgT_ev", "gback_mm"))
        score_mm, exp_ok, pv_mm, ot_ev, back_mm, norm_ok = (
            sem(n) for n in ("score_mm", "exp_ok", "pv_mm", "ot_ev", "back_mm", "norm_ok"))
        aT_mm, aT_ev, proj_mm, var_ok, rstd_ok, h1_ok = (
            sem(n) for n in ("aT_mm", "aT_ev", "proj_mm", "var_ok", "rstd_ok", "h1_ok"))
        h1T_mm, h1T_ev, gate_mm, gate_sub, gate_exp, oh_ok, cum_mm, idx_ok = (
            sem(n) for n in ("h1T_mm", "h1T_ev", "gate_mm", "gate_sub", "gate_exp", "oh_ok", "cum_mm", "idx_ok"))
        scattered = sem("scattered")
        N_LOADS = 14
        dve_own = sem("dve_own")
        passed = sem("passed")
        h1x_ok = sem("h1x_ok")
        mean2_ok, centred2, square2_ok, out2_ok, var2_ok, rstd2_ok, stored = (
            sem(n) for n in ("mean2_ok", "centred2", "square2_ok", "out2_ok", "var2_ok", "rstd2_ok", "stored"))
        w_in = [sem(f"w_in{i}") for i in range(2)]
        xT_mm, xT_ev, l1_mm, hid_ev, l2_mm, resT_ev, rback_mm, res_ok = (
            sem(n) for n in ("xT_mm", "xT_ev", "l1_mm", "hid_ev", "l2_mm", "resT_ev", "rback_mm", "res_ok"))
        fvar_ok, frstd_ok, fin_ok = (sem(n) for n in ("fvar_ok", "frstd_ok", "fin_ok"))
        out_in = [sem(f"out_in{i}") for i in range(2)]
        W_LOADS = 16 * 6

        xv = x.rearrange("b c (n f t) v -> b f c n (t v)", f=2, t=TT)
        outv = out.rearrange("b (t p) d -> b p t d", p=P)
        outrows = out.rearrange("b l d -> (b l) d")

        def apart(eng):
            eng.sem_inc(passed, 1)

        block = ctx.enter_context(nc.Block())

        @block.sync
        def _(sp):
            def load_x(b):
                for f in range(2):
                    half = slice(f * CH, (f + 1) * CH)
                    sp.dma_start(xt[half, 0:NP, :, :].rearrange("c n t v -> c n (t v)"), xv[b, f]).then_inc(x_in, 16)
                    sp.dma_start(xt[half, NP, :, :],
                                 x[b, :, TIME - 1:TIME, :].to_broadcast([CH, TT, V])).then_inc(x_in, 16)

            sp.dma_start(wl, w_tok.rearrange("d (r c) -> r d c", c=CH)).then_inc(tables_in, 16)
            sp.dma_start(cst[:, :], consts).then_inc(tables_in, 16)
            load_x(0)
            for k in range(2):
                half = slice(k * D, (k + 1) * D)
                sp.dma_start(wqk[half, :], w_qkv[:, 0:2 * D]).then_inc(loaded, 16)
                sp.dma_start(wv[half, :], w_qkv[:, 2 * D:3 * D]).then_inc(loaded, 16)
            for k in range(2):
                half = slice(k * D, (k + 1) * D)
                sp.dma_start(wp2[half, k, :], w_proj).then_inc(loaded, 16)
                sp.dma_start(wg2[half, k, :], gate_w).then_inc(loaded, 16)
                sp.dma_start(bp2[half, :], b_proj.rearrange("(p a) -> p a", a=1)).then_inc(loaded, 16)
                sp.dma_start(bv2[half, :], b_qkv[2 * D:3 * D].rearrange("(p a) -> p a", a=1)).then_inc(loaded, 16)
            sp.dma_start(bg2[:, :], gate_b.partition_broadcast(P)).then_inc(loaded, 16)
            sp.dma_start(qk_b[:, :], b_qkv[0:2 * D].rearrange("(p a) -> p a", a=1)).then_inc(loaded, 16)

            def place_parts(b):
                parts = (qk_hi, qk_lo)
                n = P // 4
                for part in range(2):
                    sp.wait_ge(parts_ok, 2 * b + 1 + part)
                    for a in (part, part + 2):
                        for g in range(HG):
                            sp.dma_start(q16[a * n:(a + 1) * n, g, :],
                                         parts[part][g * n:(g + 1) * n, R:R + L]).then_inc(q16_in, 16)
                for a in range(4):
                    rows = slice(a * n, (a + 1) * n)
                    for g in range(HG):
                        sp.dma_start(k16[rows, g, :], parts[a // 2][D + g * n:D + (g + 1) * n, :]).then_inc(k16_in, 16)

            def place_queries(b):
                need(sp, score_mm, NT * b)
                q32 = qk32[:, :, :].rearrange("p t q -> p (t q)")
                for h in range(H):
                    rows = slice(h * HD, (h + 1) * HD)
                    sp.dma_start(qd32[rows, h, :], q32[rows, R:R + L]).then_inc(q32_in, 16)

            def place_maxima(b):
                sp.wait_ge(mrow_ev, b + 1)
                for k in range(2):
                    sp.dma_start(mneg[k:k + 1, :, :], mrow[k * H:(k + 1) * H, :]).then_inc(mneg_in, 16)

            def store(b):
                sp.wait_ge(out2_ok, b + 1)
                sp.dma_start(outv[b], out2[:, :, :]).then_inc(stored, 16)

            sp.wait_ge(ready_p, 2)
            n = 32 * P
            for k in range(E * CAP // n):
                sp.dma_start(slots[k * n:(k + 1) * n, :].rearrange("(p r) c -> p (r c)", p=P),
                             fill.rearrange("p r c -> p (r c)")).then_inc(zeroed, 16)
            sp.wait_ge(tok_mm, 1)
            load_x(1)
            place_parts(0)
            sp.wait_ge(ready_v, 1)
            sp.wait_ge(ready_p, 4)
            place_queries(0)

            def body(b, first=False, last=False):
                place_maxima(b)
                if not last:
                    sp.wait_ge(tok_mm, b + 2)
                    if not (isinstance(b, int) and b + 2 >= B):
                        load_x(b + 2)
                    place_parts(b + 1)
                if not first:
                    store(b - 1)
                if not last:
                    place_queries(b + 1)

            body(0, first=True)
            with sp.Fori(1, B - 2) as b:
                body(b)
            body(B - 2)
            body(B - 1, last=True)
            def weights_in(k, e):
                sp.dma_start(w1s[k][0:D, :], w1[e]).then_inc(w_in[k], 16)
                sp.dma_start(w1s[k][D:D + 1, :], b1[bass.ds(e, 1), :]).then_inc(w_in[k], 16)
                sp.dma_start(w2s[k], w2[e].rearrange("(f p) d -> p f d", p=P)).then_inc(w_in[k], 16)
                for o in range(2):
                    sp.dma_start(b2s[k][o * D:(o + 1) * D, :], b2[e].rearrange("(d a) -> d a", a=1)).then_inc(w_in[k], 16)

            def slots_in(k, e):
                sp.dma_start(xin[k][:, :, :], slots[bass.ds(e * CAP, CAP), :].rearrange(
                    "(p i) c -> p i c", i=SE)).then_inc(w_in[k], 16)

            def experts(pair):
                for k in range(2):
                    sp.wait_ge(fin_ok, (pair * 2 + k - 1) * NSTEP)
                    slots_in(k, pair * 2 + k)
                    weights_in(k, pair * 2 + k)

            sp.wait_ge(ready_v, 2)
            weights_in(0, 0)
            sp.wait_ge(scattered, 16 * B * TOK)
            for k in range(2):
                slots_in(k, k)
            weights_in(1, 1)
            store(B - 1)
            with sp.Fori(1, E // 2) as pair:
                experts(pair)
            for k in range(2):
                sp.wait_ge(out_in[k], 16 * SI * E * NSTEP // 2)

        @block.tensor
        def _(pe):
            mm = nc.tensor.matmul

            pe.wait_ge(tables_in, 32)
            for d in range(D):
                i = mm(ps[0:D, d * PATCH // 512, d * PATCH % 512:d * PATCH % 512 + PATCH],
                       wl[:, d, :], const("dft", slice(0, 2 * F)), start=True, stop=True)
            i.then_inc(dft_mm, 1)
            pe.wait_ge(w_ready, 4)

            hflat = hcat[:, :, :].rearrange("p t q -> p (t q)")
            turn = nc.tensor.transpose

            def tokens(b, first, last):
                for n in range(first, last):
                    k, t = divmod(n, TT)
                    if n == 0:
                        pe.wait_ge(x_in, 64 * b + 64)
                        need(pe, qk_ev, b)
                    mm(ps[:, 6 + k, :], wtok[:, t, :, :].rearrange("p s d -> p (s d)"),
                       xt[:, k * 8:(k + 1) * 8, t, :], start=(t == 0), stop=(t == TT - 1))

            def tokens_padding(b):
                for t in range(TT):
                    i = mm(ps[D:P, 4, P:P + V], wtok[:, t, 1, :], xt[:, NP, t, :], start=(t == 0), stop=(t == TT - 1))
                i.then_inc(tok_mm, 1)

            def queries_keys(b):
                pe.wait_ge(hcat_lo, b + 1)
                pe.wait_ge(hcat_hi, 2 * b + 2)
                for k in range(2):
                    i = mm(ps[:, 6 + k, :], wqk[:, :], hflat[:, R + 512 * k:R + 512 * (k + 1)], start=True, stop=True)
                i.then_inc(qk_mm, 1)

            def maxima(b, c):
                if c == 0:
                    pe.wait_ge(k16_in, 128 * b + 128)
                    need(pe, v_ev, 5 * b)
                if c % (NC // QSTEPS) == 0:
                    pe.wait_ge(qd16_ok, QSTEPS * b + c // (NC // QSTEPS) + 1)
                    pe.wait_ge(qd16_last, HG * (QSTEPS * b + c // (NC // QSTEPS) + 1))
                if c >= 2:
                    pe.wait_ge(max_rd, NC * b + c - 1)
                for n in range(GC * HG):
                    g, a = GC * c + n // HG, n % HG
                    i = mm(ps[:, 2 + c % 2, n * GK:(n + 1) * GK], qd16[:, g, a, :, :].rearrange("p h j -> p (h j)"),
                           k16[:, a, g * G:g * G + GK], start=True, stop=True)
                i.then_inc(max_mm, 1)

            def maxima_rows(b):
                need(pe, exp_ok, NT * b)
                need(pe, yT_ev, b)
                for k in range(2):
                    pe.wait_ge(spread_ok, 4 * b + 2 * k + 2)
                    for n in range(2 * HG):
                        o, a = n // HG, n % HG
                        i = mm(ps[0:2 * H, k, :], sel16[:, 16 * n:16 * n + 16],
                               spread[o][:, k, a * NG // 2:(a + 1) * NG // 2, :].rearrange("p g j -> p (g j)"),
                               start=(n == 0), stop=(n == 2 * HG - 1))
                i.then_inc(mrow_mm, 1)

            def values(b):
                pe.wait_ge(max_rd, NC * b + NC)
                need(pe, centred, b)
                xeven = hcat[:, 0:TOK, :].rearrange("p (t o) q -> p o t q", o=2)
                teven = hflat[:, R:R + L].rearrange("p (t o q) -> p o t q", o=2, q=P)
                for o in range(2):
                    mm(ps[o * D:(o + 1) * D, 2, :], wv[:, :], xeven[:, o], start=True, stop=True)
                mm(ps[0:D, 4, 0:P], wv[:, :], hcat[:, TOK, :], start=True, stop=True)
                for o in range(2):
                    i = mm(ps[o * D:(o + 1) * D, 3, :], const("fold"), teven[:, o], start=True, stop=True)
                i.then_inc(vh_mm, 1)

            def values_back(b):
                pe.wait_ge(vT_ev, 3 * b + 3)
                apart(pe)
                for t in range(TOK // 2):
                    turn(ps[:, 2, t * P:(t + 1) * P], vT[:, t, :], ident)

            def values_back_last(b):
                pe.wait_ge(h_ev, b + 1)
                apart(pe)
                turn(ps[:, 3, 0:D], vT_last[:, :], cst[0:D, COL["ident"][0]:COL["ident"][0] + D]).then_inc(vback_mm, 1)

            def scores(b, t):
                if t == 0:
                    pe.wait_ge(kwin_ok, 4 * b + 4)
                    pe.wait_ge(q32_in, 128 * b + 128)
                    pe.wait_ge(mneg_in, 32 * b + 32)
                if t >= 2:
                    pe.wait_ge(exp_ok, NT * b + t - 1)
                o = ps[:, t % 2, :]
                cols = slice(t * QT, (t + 1) * QT)
                mm(o, kwin[:, t, :], qd32[:, :, cols], start=True, stop=False)
                mm(o, ones16[:, :], mneg[:, :, cols], start=False, stop=True).then_inc(score_mm, 1)

            def weighted(b, t, front):
                if t == 0:
                    pe.wait_ge(v_ev, 5 * b + 5)
                    if front:
                        pe.wait_ge(hcat_hi, 2 * b + 4)
                if t % 4 == 0 and t:
                    pe.wait_ge(ot_ev, QUADS * b + t // 4)
                pe.wait_ge(exp_ok, NT * b + t + 1)
                for c in range(4):
                    i = mm(ps[32 * c:32 * c + 32, 4, (t % 4) * P:(t % 4 + 1) * P],
                           vals[t % 2][:, t // 2, 2 * c:2 * c + 2, :].rearrange("p h w -> p (h w)"),
                           probs[:, t % 3, 2 * c:2 * c + 2, :].rearrange("p h q -> p (h q)"), start=True, stop=True)
                i.then_inc(pv_mm, 1)

            def turn_back(b, k):
                pe.wait_ge(ot_ev, QUADS * b + k + 1)
                need(pe, norm_ok, QUADS * b + k)
                if k == 0:
                    need(pe, idx_ok, b)
                apart(pe)
                for s in range(4):
                    i = turn(ps[:, 5, s * P:(s + 1) * P], ot[:, k % 2, s, :], ident)
                i.then_inc(back_mm, 1)

            def attended_T(b):
                pe.wait_ge(norm_ok, QUADS * b + QUADS)
                pe.wait_ge(exp_ok, NT * b + NT)
                apart(pe)
                for t in range(TOK // 2):
                    i = turn(ps[:, 0, t * P:(t + 1) * P], atok[:, 2 * t:2 * t + 2, :].rearrange("p t d -> p (t d)"), ident)
                i.then_inc(aT_mm, 1)

            def projection(b):
                pe.wait_ge(aT_ev, b + 1)
                for o in range(2):
                    i = mm(ps[o * D:(o + 1) * D, 1, :], wp2[:, o, :], aT[:, :], start=True, stop=True)
                i.then_inc(proj_mm, 1)

            def rows_back(b):
                pe.wait_ge(yT_ev, b + 1)
                apart(pe)
                for t in range(TOK // 2):
                    i = turn(ps[:, 4, t * P:(t + 1) * P], yT[:, t * P:(t + 1) * P], ident)
                i.then_inc(yback_mm, 1)

            def normed_T(b):
                pe.wait_ge(h1_ok, b + 1)
                apart(pe)
                for t in range(TOK // 2):
                    i = turn(ps[:, 5, t * P:(t + 1) * P], h1[:, 2 * t:2 * t + 2, :].rearrange("p t d -> p (t d)"), ident)
                i.then_inc(h1T_mm, 1)

            def gate(b):
                pe.wait_ge(h1T_ev, b + 1)
                mm(ps[0:2 * E, 5, :], wg2[:, :, :].rearrange("p o e -> p (o e)"), h1T[:, :],
                   start=True, stop=True).then_inc(gate_mm, 1)

            def gate_back(b):
                pe.wait_ge(lgT_ev, b + 1)
                apart(pe)
                for t in range(TOK // 2):
                    i = turn(ps[:, 5, 2 * E * t:2 * E * (t + 1)], lgT[:, t * P:(t + 1) * P],
                             cst[0:2 * E, COL["ident"][0]:COL["ident"][0] + 2 * E])
                i.then_inc(gback_mm, 1)

            def counts(b):
                pe.wait_ge(oh_ok, b + 1)
                for s in range(1, TOK + 1):
                    mm(ps[:, 5, CNT + s * E:CNT + (TOK + 1) * E], ones16[:, :],
                       oh16[:, 0:TOK + 1 - s, :].rearrange("p t e -> p (t e)"),
                       start=(s == 1), stop=False, skip_group_check=True)
                mm(ps[:, 5, CNT:CNT + TOK * E], before16[:, :], oh16[:, 0:TOK, :].rearrange("p t e -> p (t e)"),
                   start=False, stop=True, skip_group_check=True).then_inc(cum_mm, 1)

            tokens(0, 0, 2 * TT)
            tokens_padding(0)
            pe.wait_ge(loaded, 16 * N_LOADS)
            pe.wait_ge(ready_v, 1)
            pe.wait_ge(ready_a, 2)
            queries_keys(0)
            tokens(1, 0, sum(TOKENS_LAST))
            for c in range(NC):
                maxima(0, c)

            def body(b, first=False, last=False, ahead=True):
                maxima_rows(b)
                values(b)
                if not last:
                    tokens(b + 1, sum(TOKENS_LAST), 2 * TT)
                    tokens_padding(b + 1)
                values_back(b)
                if not first:
                    normed_T(b - 1)
                if not last:
                    queries_keys(b + 1)
                values_back_last(b)
                if not first:
                    gate(b - 1)
                chunks = iter(() if last else range(NC))

                def more(n):
                    for _ in range(n):
                        c = next(chunks, None)
                        if c is not None:
                            maxima(b + 1, c)

                for t in range(NT):
                    scores(b, t)
                    if t == 0 and not first:
                        gate_back(b - 1)
                    if t == 3 and not first:
                        counts(b - 1)
                    if t:
                        weighted(b, t - 1, not last)
                    if t % 4 == 1 and t > 4:
                        turn_back(b, t // 4 - 1)
                    more(AFTER_TILE[t])
                def step(n):
                    more(AFTER_LAST[n])
                    if ahead:
                        tokens(b + 2, sum(TOKENS_LAST[:n]), sum(TOKENS_LAST[:n + 1]))

                weighted(b, NT - 1, not last)
                step(0)
                turn_back(b, QUADS - 1)
                step(1)
                attended_T(b)
                step(2)
                projection(b)
                step(3)
                rows_back(b)
                step(4)

            body(0, first=True)
            with pe.Fori(1, B - 2) as b:
                body(b)
            body(B - 2, ahead=False)
            body(B - 1, last=True, ahead=False)
            normed_T(B - 1)
            gate(B - 1)
            gate_back(B - 1)
            counts(B - 1)

            pe.wait_ge(idx_ok, B)
            pe.wait_ge(ready_v, 2)

            def turn_slots(pair, n):
                k = n // NSTEP
                if n % NSTEP == 0:
                    pe.wait_ge(w_in[k], W_LOADS * (pair + 1))
                apart(pe)
                for i in range(SI):
                    ins = turn(ps[0:D, n % 2, i * P:(i + 1) * P], xin[k][:, n % NSTEP * SI + i, 0:D], ident)
                ins.then_inc(xT_mm, 1)

            def layer1(pair, n):
                step = pair * 2 * NSTEP + n
                k = n // NSTEP
                pe.wait_ge(xT_ev, step + 1)
                need(pe, hid_ev, 2 * (step - 1))
                for f in range(2):
                    i = mm(ps[:, 2 + 2 * (n % 2) + f, :], w1s[k][:, f * P:(f + 1) * P], xinT[n % 2], start=True, stop=True)
                i.then_inc(l1_mm, 1)

            def layer2(pair, n):
                step = pair * 2 * NSTEP + n
                k = n // NSTEP
                pe.wait_ge(hid_ev, 2 * step + 2)
                need(pe, resT_ev, step)
                for f in range(2):
                    for o in range(2):
                        ins = mm(ps[o * D:(o + 1) * D, 6, 0:SL // 2], w2s[k][:, f, :],
                                 hid[n % 2][:, f, :].rearrange("p (i o s) -> p o i s", o=2, s=P)[:, o],
                                 start=(f == 0), stop=(f == 1), skip_group_check=True)
                ins.then_inc(l2_mm, 1)

            def results_back(step):
                pe.wait_ge(resT_ev, step + 1)
                need(pe, res_ok, step)
                apart(pe)
                for i in range(SI // 2):
                    ins = turn(ps[:, 7, i * P:(i + 1) * P], resT[:, i * P:(i + 1) * P], ident)
                ins.then_inc(rback_mm, 1)

            def experts(pair):
                step = pair * 2 * NSTEP
                turn_slots(pair, 0)
                for n in range(2 * NSTEP):
                    layer1(pair, n)
                    if n + 1 < 2 * NSTEP:
                        turn_slots(pair, n + 1)
                    if n:
                        results_back(step + n - 1)
                    layer2(pair, n)
                results_back(step + 2 * NSTEP - 1)

            experts(0)
            with pe.Fori(1, E // 2) as pair:
                experts(pair)

        @block.scalar
        def _(act):
            act.wait_ge(tables_in, 32)
            act.wait_ge(loaded, 16 * N_LOADS)
            nc.scalar.activation(qk_bias[:, :], qk_b[:, :], ACT.Identity, scale=qk_scale).then_inc(ready_a, 1)
            nc.scalar.activation(sel16[:, :], const("sel"), ACT.Copy).then_inc(ready_a, 1)
            act.wait_ge(ready_a, 2)
            act.wait_ge(ready_v, 1)
            hflat = hcat[:, :, :].rearrange("p t q -> p (t q)")
            q32 = qk32[:, :, :].rearrange("p t q -> p (t q)")
            vflat = vT[:, :, :].rearrange("p t q -> p (t q)")

            def tokens_low(b):
                act.wait_ge(tok_mm, b + 1)
                nc.scalar.activation(hflat[0:D, R:R + L].rearrange("p (v n) -> p v n", n=NP),
                                     ps[0:D, 6:8, :].rearrange("p k (n v) -> p v (k n)", v=V),
                                     ACT.Copy).then_inc(hcat_lo, 1)

            def queries_keys(b):
                act.wait_ge(qk_mm, b + 1)
                need(act, q32_in, 128 * b)
                need(act, kwin_ok, 4 * b)
                nc.scalar.activation(q32[:, R:R + L], ps[:, 6:8, :].rearrange("p k q -> p (k q)"), ACT.Identity,
                                     bias=qk_bias[:, :], scale=qk_scale).then_inc(qk_ev, 1)

            def values(b):
                act.wait_ge(vh_mm, b + 1)
                need(act, vback_mm, b)
                for dst, src, rows in ((vflat[0:D, R:], ps[0:D, 2, R:], slice(0, D)), (vflat[D:P, :], ps[D:P, 2, :], slice(D, P)),
                                       (vT_last[:, 0:R], ps[0:D, 4, 0:R], slice(0, D))):
                    nc.scalar.activation(dst, src, ACT.Identity, bias=bv2[rows, :]).then_inc(vT_ev, 1)

            def own_tokens(b):
                need(act, yT_ev, b)
                nc.scalar.activation(hT[:, :], ps[:, 3, :], ACT.Copy).then_inc(h_ev, 1)

            def normed_T(b):
                act.wait_ge(h1T_mm, b + 1)
                need(act, gate_mm, b)
                nc.scalar.activation(h1T[:, :], ps[:, 5, :], ACT.Copy).then_inc(h1T_ev, 1)

            def payload(b):
                act.wait_ge(h1_ok, b + 1)
                need(act, scattered, 16 * TOK * b)
                nc.scalar.activation(h1x[:, :, 0:D], h1[:, :, :], ACT.Copy).then_inc(h1x_ok, 1)

            def logits_T(b):
                act.wait_ge(gate_mm, b + 1)
                need(act, gback_mm, b)
                nc.scalar.activation(lgT[:, :], ps[0:2 * E, 5, :], ACT.Copy).then_inc(lgT_ev, 1)

            def gate_weights(b):
                act.wait_ge(gate_sub, b + 1)
                nc.scalar.activation(ex[:, :, :], lg[:, :, :], ACT.Exp).then_inc(gate_exp, 1)

            def sums_out(b, k):
                act.wait_ge(pv_mm, NT * b + 4 * k + 4)
                need(act, back_mm, QUADS * b + k - 1)
                nc.scalar.activation(ot[:, k % 2, :, :].rearrange("p s c -> p (s c)"), ps[:, 4, :],
                                     ACT.Copy).then_inc(ot_ev, 1)

            def diagonal(b, k, a):
                act.wait_ge(q16_in, 128 * b + 128)
                need(act, max_mm, NC * b)
                if isinstance(b, int) and b == 0:
                    act.wait_ge(zeroed, 80)
                n, h = NG // QSTEPS, HW - 1
                nc.scalar.activation(qd16[:, k * n:(k + 1) * n, a, h, :],
                                     q16[:, a, k * n * G:(k + 1) * n * G].rearrange("p (g j) -> p g j", j=G),
                                     ACT.Identity, scale=cst[:, COL["heads"][0] + h:COL["heads"][0] + h + 1]
                                     ).then_inc(qd16_last, 1)

            def windows(b):
                act.wait_ge(qk_ev, b + 1)
                need(act, score_mm, NT * b)
                kw = kwin[0:D, :, :].rearrange("p (t o) (f k) -> p o f t k", o=2, f=2)
                for o, f, t0, f0 in ((0, 0, 0, 0), (0, 1, 0, 1), (1, 1, 0, 1), (1, 0, 1, 0)):
                    nc.scalar.activation(kw[:, o, f], qk32[D:P, t0:t0 + TOK, f0 * QT:(f0 + 1) * QT], ACT.Copy).then_inc(kwin_ok, 1)

            tokens_low(0)
            queries_keys(0)
            for m in range(QSTEPS * HG):
                diagonal(0, m // HG, m % HG)
            windows(0)

            def body(b, first=False, last=False):
                values(b)
                if not last:
                    tokens_low(b + 1)
                own_tokens(b)
                if not first:
                    normed_T(b - 1)
                if not last:
                    queries_keys(b + 1)
                if not first:
                    logits_T(b - 1)
                for t in range(NT):
                    act.wait_ge(score_mm, NT * b + t + 1)
                    need(act, pv_mm, NT * b + t - 2)
                    nc.scalar.activation(probs[:, t % 3, :, :].rearrange("p h q -> p (h q)"), ps[:, t % 2, :],
                                         ACT.Exp).then_inc(exp_ok, 1)
                    if t == 2 and not first:
                        gate_weights(b - 1)
                    if t == 1 and not first:
                        payload(b - 1)
                    if t in DIAGONAL_TILES and not last:
                        diagonal(b + 1, *divmod(DIAGONAL_TILES.index(t), HG))
                    if t % 4 == 0 and t:
                        sums_out(b, t // 4 - 1)
                sums_out(b, QUADS - 1)
                act.wait_ge(aT_mm, b + 1)
                need(act, proj_mm, b)
                nc.scalar.activation(aT[:, :], ps[:, 0, :], ACT.Copy).then_inc(aT_ev, 1)
                if not last:
                    windows(b + 1)

            body(0, first=True)
            with act.Fori(1, B - 1) as b:
                body(b)
            body(B - 1, last=True)
            normed_T(B - 1)
            payload(B - 1)
            logits_T(B - 1)
            gate_weights(B - 1)

            def slots_T(pair, n):
                step = pair * 2 * NSTEP + n
                act.wait_ge(xT_mm, step + 1)
                need(act, l1_mm, step - 1)
                nc.scalar.activation(xinT[n % 2][0:D, :], ps[0:D, n % 2, :], ACT.Copy).then_inc(xT_ev, 1)

            def experts(pair):
                slots_T(pair, 0)
                for n in range(2 * NSTEP):
                    step = pair * 2 * NSTEP + n
                    act.wait_ge(l1_mm, step + 1)
                    need(act, l2_mm, step - 1)
                    for f in range(2):
                        nc.scalar.activation(hid[n % 2][:, f, :], ps[:, 2 + 2 * (n % 2) + f, :], ACT.Relu).then_inc(hid_ev, 1)
                    if n + 1 < 2 * NSTEP:
                        slots_T(pair, n + 1)
                    act.wait_ge(l2_mm, step + 1)
                    need(act, rback_mm, step)
                    nc.scalar.activation(resT, ps[:, 6, 0:SL // 2], ACT.Identity, bias=b2s[n // NSTEP]).then_inc(resT_ev, 1)

            experts(0)
            with act.Fori(1, E // 2) as pair:
                experts(pair)

        @block.gpsimd
        def _(pool):
            nc.gpsimd.memset(fill.rearrange("p r c -> p (r c)"), 0.0).then_inc(ready_p, 1)
            pool.wait_ge(ready_p, 1)
            nc.gpsimd.memset(fill[:, :, D:D + 1], float(NOBODY)).then_inc(ready_p, 1)
            nc.gpsimd.memset(place[0:D, :], 0.0).then_inc(ready_p, 1)
            pool.wait_ge(dft_mm, 1)
            nc.gpsimd.memset(mneg[:, :, :].rearrange("p h q -> p (h q)"), 0.0).then_inc(ready_p, 1)
            pool.wait_ge(tables_in, 32)

            def spread_maxima(b, k):
                need(pool, mrow_mm, b)
                n = HG * NG // 2
                for o, part in enumerate((mx_hi, mx_lo)):
                    pool.wait_ge(mx_ok, 4 * b + 2 * k + 1 + o)
                    nc.gpsimd.tensor_tensor(
                        spread[o][:, k, :, :],
                        part[:, k, :, :].rearrange("p a g -> p (a g)").unsqueeze(2).to_broadcast([P, n, G]),
                        const("delta").unsqueeze(1).to_broadcast([P, n, G]), ALU.mult).then_inc(spread_ok, 1)

            def inv_std(src, dst, ready, done, n):
                pool.wait_ge(ready, n)
                nc.gpsimd.tensor_tensor(dst, src, minus_half.to_broadcast([P, dst.shape[1]]), ALU.pow).then_inc(done, 1)

            def second_squares(b):
                pool.wait_ge(mean2_ok, b + 1)
                nc.gpsimd.tensor_tensor(yc[:, :, :], h1[:, :, :], st[:, 7, :].unsqueeze(2).to_broadcast([P, TOK, D]),
                                        ALU.subtract).then_inc(centred2, 1)
                pool.wait_ge(centred2, b + 1)
                nc.gpsimd.tensor_tensor(sq[:, :, :], yc[:, :, :], yc[:, :, :], ALU.mult).then_inc(square2_ok, 1)

            def second_norm(b):
                inv_std(st[:, 5, :], st[:, 6, :], var2_ok, rstd2_ok, b + 1)
                pool.wait_ge(rstd2_ok, b + 1)
                need(pool, stored, 16 * b)
                nc.gpsimd.tensor_tensor(out2[:, :, :], yc[:, :, :], st[:, 6, :].unsqueeze(2).to_broadcast([P, TOK, D]),
                                        ALU.mult).then_inc(out2_ok, 1)

            def scatter(b):
                pool.wait_ge(h1x_ok, b + 1)
                pool.wait_ge(idx_ok, b + 1)
                apart(pool)
                for t in range(TOK):
                    nc.gpsimd.indirect_dma_start(
                        out=slots, out_offset=bass.IndirectOffsetOnAxis(ap=sidx[:, t:t + 1], axis=0),
                        in_=h1x[:, t, :], in_offset=None).then_inc(scattered, 16)

            pool.wait_ge(zeroed, 80)
            for k in range(2):
                spread_maxima(0, k)

            def body(b, first=False, last=False):
                if not first:
                    second_norm(b - 1)
                    scatter(b - 1)
                if not last:
                    spread_maxima(b + 1, 0)
                    spread_maxima(b + 1, 1)
                inv_std(st[:, 1, :], st[:, 2, :], var_ok, rstd_ok, b + 1)
                second_squares(b)

            body(0, first=True)
            with pool.Fori(1, B - 1) as b:
                body(b)
            body(B - 1, last=True)
            scatter(B - 1)
            second_norm(B - 1)

            pool.wait_ge(stored, 16 * B)

            def scatter_out(step, n):
                pool.wait_ge(fin_ok, step + 1)
                apart(pool)
                for i in range(SI):
                    c = n % NSTEP * SI + i
                    nc.gpsimd.indirect_dma_start(
                        out=outrows, out_offset=bass.IndirectOffsetOnAxis(ap=ids[n // NSTEP][:, c:c + 1], axis=0),
                        in_=fin[n % 2][:, i, :], in_offset=None, bounds_check=B * L - 1, oob_is_err=False
                    ).then_inc(out_in[n % 2], 16)

            def experts(pair, first=False):
                step = pair * 2 * NSTEP
                for n in range(2 * NSTEP):
                    inv_std(fst[:, 1, :], fst[:, 2, :], fvar_ok, frstd_ok, step + n + 1)
                    if not (first and n == 0):
                        scatter_out(step + n - 1, (n - 1) % (2 * NSTEP))

            experts(0, first=True)
            with pool.Fori(1, E // 2) as pair:
                experts(pair)
            scatter_out(E * NSTEP - 1, 2 * NSTEP - 1)

        @block.vector
        def _(dve):
            own = Chain(dve, dve_own)
            link = own.link
            v = nc.vector
            dve.wait_ge(tables_in, 32)

            link(v.memset(hcat[:, :, :].rearrange("p t q -> p (t q)"), 0.0))
            link(v.memset(qk32[:, :, :].rearrange("p t q -> p (t q)"), 0.0))
            dve.wait_ge(dft_mm, 1)
            wps = ps[0:D, 0:2, :].rearrange("p k (d t) -> p (k d) t", t=PATCH)
            for f in range(2):
                half = slice(f * CH, (f + 1) * CH)
                for s in range(2):
                    t0 = s * STRIDE + f * TT
                    v.tensor_copy(wtok[half, :, s, :], wps[:, :, t0:t0 + TT].rearrange("p d t -> p t d")
                                  ).then_inc(w_ready, 1)

            link(v.tensor_copy(place[D:P, :].rearrange("p (n j) -> p n j", j=QT),
                               const("onehot", slice(D, P)).unsqueeze(1).to_broadcast([D, H * L // QT, QT])))
            link(v.memset(vT[0:D, 0, 0:R], 0.0))
            link(v.memset(vT_last[:, :], 0.0))
            for w in (wp2, wg2):
                for k in range(2):
                    link(v.memset(w[k * D:(k + 1) * D, 1 - k, :], 0.0))
            link(v.memset(ones16[:, :], 1.0))
            link(v.tensor_copy(before16[:, :], const("before")))
            link(v.memset(oh16[:, :, :].rearrange("p t e -> p (t e)"), 0.0))
            link(v.memset(run[:, :], 0.0))
            link(v.tensor_copy(number[:, :], const("number")))
            for o in range(2):
                link(v.tensor_copy(kwin[D:P, :, :].rearrange("p (t o) k -> p o t k", o=2)[:, o],
                                   cst[D:P, COL["keymask"][0] + o * P:COL["keymask"][0] + (o + 1) * P]
                                   .unsqueeze(1).to_broadcast([D, NT // 2, P])))
            v.nop().then_inc(ready_v, 1)

            hflat = hcat[:, :, :].rearrange("p t q -> p (t q)")
            q32 = qk32[:, :, :].rearrange("p t q -> p (t q)")

            def tokens_high(b):
                dve.wait_ge(tok_mm, b + 1)
                hv = hflat[D:P, R:R + L].rearrange("p (v n) -> p v n", n=NP)
                v.tensor_copy(hv[:, :, 0:NP - 1],
                              ps[D:P, 6:8, :].rearrange("p k (n v) -> p v (k n)", v=V)[:, :, 1:NP]).then_inc(hcat_hi, 1)
                v.tensor_copy(hv[:, :, NP - 1:NP], ps[D:P, 4, P:P + V].unsqueeze(2)).then_inc(hcat_hi, 1)

            def parts(b):
                dve.wait_ge(qk_ev, b + 1)
                need(dve, q16_in, 128 * b)
                need(dve, k16_in, 128 * b)
                v.tensor_copy(qk_hi[:, :], q32[:, 0:XP]).then_inc(parts_ok, 1)
                dve.wait_ge(parts_ok, 2 * b + 1)
                v.tensor_tensor(qk_lo[:, :], q32[:, 0:XP], qk_hi[:, :], ALU.subtract).then_inc(parts_ok, 1)

            def diagonal(b):
                dve.wait_ge(q16_in, 128 * b + 128)
                need(dve, max_mm, NC * b)
                if isinstance(b, int) and b == 0:
                    dve.wait_ge(zeroed, 80)
                n = NG // QSTEPS
                for k in range(QSTEPS):
                    for a in range(HG):
                        src = q16[:, a, k * n * G:(k + 1) * n * G].rearrange("p (g j) -> p g j", j=G)
                        for h in range(HW - 1):
                            i = v.tensor_scalar(qd16[:, k * n:(k + 1) * n, a, h, :], src,
                                                cst[:, COL["heads"][0] + h:COL["heads"][0] + h + 1], None, ALU.mult)
                    i.then_inc(qd16_ok, 1)

            def maxima(b, c):
                need(dve, max_rd, NC * b + c - 1)
                dve.wait_ge(max_mm, NC * b + c + 1)
                apart(dve)
                for n in range(GC * HG):
                    g, a = GC * c + n // HG, n % HG
                    k, g = divmod(g, NG // 2)
                    i = v.tensor_tensor_reduce(junk[:, c % 2 * GC * HG + n, :], ps[:, 2 + c % 2, n * GK:(n + 1) * GK],
                                               const("winmask"), 1.0, -3e38, ALU.add, ALU.max, mx[:, k, a, g:g + 1])
                i.then_inc(max_rd, 1)

            def maxima_rows(b):
                dve.wait_ge(mrow_mm, b + 1)
                need(dve, mneg_in, 32 * b)
                v.tensor_copy(mrow[:, :], ps[0:2 * H, 0:2, :].rearrange("p k q -> p (k q)")).then_inc(mrow_ev, 1)

            def maxima_parts(b, k):
                dve.wait_ge(max_rd, NC * b + (k + 1) * NC // 2)
                need(dve, spread_ok, 4 * b)
                v.tensor_scalar(mx_hi[:, k], mx[:, k], -1.0, None, ALU.mult).then_inc(mx_ok, 1)
                dve.wait_ge(mx_ok, 4 * b + 2 * k + 1)
                link(v.tensor_tensor(mx_rest[:, k], mx[:, k], mx_hi[:, k], ALU.add))
                v.tensor_scalar(mx_lo[:, k], mx_rest[:, k], -1.0, None, ALU.mult).then_inc(mx_ok, 1)

            def values(b):
                dve.wait_ge(vback_mm, b + 1)
                pv = ps[:, 2, :].rearrange("p (t h d) -> p t h d", h=H, d=HD)
                p9 = ps[:, 3, 0:D].rearrange("p (t h d) -> p t h d", t=1, d=HD)
                e, o = (u[:, :, :, 0:HD] for u in vals)
                v.tensor_copy(e, pv).then_inc(v_ev, 1)
                v.tensor_copy(o[D:P], pv[D:P]).then_inc(v_ev, 1)
                v.tensor_copy(o[0:D, 0:TOK - 1], pv[0:D, 1:TOK]).then_inc(v_ev, 1)
                v.tensor_copy(o[0:D, TOK - 1:TOK], p9[0:D]).then_inc(v_ev, 2)

            def normalize(b, k):
                dve.wait_ge(back_mm, QUADS * b + k + 1)
                bank = ps[:, 5, :].rearrange("p (s c h w) -> p s c h w", s=4, c=4, h=2)
                for hh in range(2):
                    half = slice(hh * D, (hh + 1) * D)
                    i = v.reciprocal(rden[half, k % 2, :, :], bank[half, :, :, hh, HD])
                link(i)
                at = atok[:, :, :].rearrange("p t (c h d) -> p t c h d", c=4, h=2)
                for hh in range(2):
                    half = slice(hh * D, (hh + 1) * D)
                    for s in range(4):
                        i = v.tensor_tensor(
                            at[(s % 2) * D:(s % 2 + 1) * D, 2 * k + s // 2, :, hh, :], bank[half, s, :, hh, 0:HD],
                            rden[half, k % 2, s, :].unsqueeze(2).to_broadcast([D, 4, HD]), ALU.mult)
                i.then_inc(norm_ok, 1)

            def bc(a, n, m=TOK):
                return a.unsqueeze(2).to_broadcast([P, m, n])

            def residual(b):
                dve.wait_ge(proj_mm, b + 1)
                dve.wait_ge(h_ev, b + 1)
                need(dve, yback_mm, b)
                v.scalar_tensor_tensor(out=yT[:, :], in0=ps[:, 1, :], scalar=bp2[:, :], in1=hT[:, :],
                                       op0=ALU.add, op1=ALU.add).then_inc(yT_ev, 1)

            def first_stats(b):
                dve.wait_ge(yback_mm, b + 1)
                need(dve, out2_ok, b)
                rows = ps[:, 4, :].rearrange("p (t d) -> p t d", d=D)
                link(v.tensor_reduce(st[:, 0, :], rows, AX, ALU.add))
                link(v.tensor_scalar(st[:, 3, :], st[:, 0, :], 1.0 / D, None, ALU.mult))
                v.tensor_tensor(yc[:, :, :], rows, bc(st[:, 3, :], D), ALU.subtract).then_inc(centred, 1)
                dve.wait_ge(centred, b + 1)
                link(v.tensor_tensor(sq[:, :, :], yc[:, :, :], yc[:, :, :], ALU.mult))
                link(v.tensor_reduce(st[:, 4, :], sq[:, :, :], AX, ALU.add))
                v.tensor_scalar(st[:, 1, :], st[:, 4, :], 1.0 / D, EPS, ALU.mult, ALU.add).then_inc(var_ok, 1)

            def first_norm(b):
                dve.wait_ge(rstd_ok, b + 1)
                need(dve, h1x_ok, b)
                need(dve, scattered, 16 * TOK * b)
                v.tensor_tensor(h1[:, :, :], yc[:, :, :], bc(st[:, 2, :], D), ALU.mult).then_inc(h1_ok, 1)
                dve.wait_ge(h1_ok, b + 1)
                link(v.tensor_scalar(h1x[:, :, D], number[:, :], 1.0, None, ALU.mult))
                link(v.tensor_scalar(number[:, :], number[:, :], float(L), None, ALU.add))

            def second_mean(b):
                link(v.tensor_reduce(st[:, 0, :], h1[:, :, :], AX, ALU.add))
                v.tensor_scalar(st[:, 7, :], st[:, 0, :], 1.0 / D, None, ALU.mult).then_inc(mean2_ok, 1)

            def second_variance(b):
                dve.wait_ge(square2_ok, b + 1)
                link(v.tensor_reduce(st[:, 4, :], sq[:, :, :], AX, ALU.add))
                v.tensor_scalar(st[:, 5, :], st[:, 4, :], 1.0 / D, EPS, ALU.mult, ALU.add).then_inc(var2_ok, 1)

            lmax, esum, prb, code, pos, ebase, kept, t0, t1, t2 = (rt[:, k, :] for k in range(10))

            def route(b):
                dve.wait_ge(gback_mm, b + 1)
                link(v.tensor_tensor(logit[:, :, :], ps[:, 5, 0:TOK * E].rearrange("p (t e) -> p t e", e=E),
                                     bg2[:, :].unsqueeze(1).to_broadcast([P, TOK, E]), ALU.add))
                link(v.tensor_reduce(lmax, logit[:, :, :], AX, ALU.max))
                v.tensor_tensor(lg[:, :, :], logit[:, :, :], bc(lmax, E), ALU.subtract).then_inc(gate_sub, 1)
                dve.wait_ge(gate_sub, b + 1)
                link(v.tensor_scalar(cand[:, :, :], lg[:, :, :], 0.0, None, ALU.is_ge))
                link(v.tensor_tensor(cand[:, :, :], cand[:, :, :],
                                     const("rev").unsqueeze(1).to_broadcast([P, TOK, E]), ALU.mult))
                link(v.tensor_reduce(code, cand[:, :, :], AX, ALU.max))
                v.tensor_tensor(oh16[:, 0:TOK, :], cand[:, :, :], bc(code, E), ALU.is_equal).then_inc(oh_ok, 1)

            def slots_of(b):
                dve.wait_ge(gate_exp, b + 1)
                link(v.tensor_reduce(esum, ex[:, :, :], AX, ALU.add))
                link(v.reciprocal(prb, esum))
                dve.wait_ge(oh_ok, b + 1)
                dve.wait_ge(cum_mm, b + 1)
                cnt = ps[:, 5, CNT:CNT + (TOK + 1) * E].rearrange("p (t e) -> p t e", e=E)
                link(v.tensor_tensor(posw[:, :, :], cnt[:, 0:TOK, :],
                                     run[:, :].unsqueeze(1).to_broadcast([P, TOK, E]), ALU.add))
                link(v.tensor_tensor(posw[:, :, :], posw[:, :, :], oh16[:, 0:TOK, :], ALU.mult))
                link(v.tensor_reduce(pos, posw[:, :, :], AX, ALU.add))
                link(v.tensor_tensor(run[:, :], cnt[:, TOK, :], run[:, :], ALU.add))
                link(v.tensor_scalar(ebase, code, float(-CAP), float(E * CAP), ALU.mult, ALU.add))
                link(v.tensor_scalar(kept, pos, float(CAP), None, ALU.is_lt))
                link(v.tensor_tensor(h1x[:, :, D + 1], prb, kept, ALU.mult))
                link(v.tensor_tensor(t0, ebase, pos, ALU.add))
                link(v.tensor_tensor(t0, t0, const("trash"), ALU.subtract))
                link(v.tensor_tensor(t0, t0, kept, ALU.mult))
                need(dve, scattered, 16 * TOK * b)
                v.tensor_tensor(sidx[:, :], t0, const("trash"), ALU.add).then_inc(idx_ok, 1)

            tokens_high(0)
            parts(0)
            diagonal(0)
            for c in range(NC):
                maxima(0, c)
                if c % (NC // 2) == NC // 2 - 1:
                    maxima_parts(0, c // (NC // 2))
            for o in range(2):
                link(v.memset(vals[o][:, :, :, :].rearrange("p t h w -> p (t h w)"), 0.0))
                link(v.memset(vals[o][:, :, :, HD:HD + 1], 1.0))

            def body(b, first=False, last=False):
                if not last:
                    tokens_high(b + 1)
                values(b)
                if not first:
                    second_variance(b - 1)
                if not last:
                    parts(b + 1)
                if not first:
                    route(b - 1)
                    slots_of(b - 1)
                chunks = iter(() if last else range(NC))

                def more(n):
                    for _ in range(n):
                        c = next(chunks, None)
                        if c is not None:
                            maxima(b + 1, c)
                            if c % (NC // 2) == NC // 2 - 1:
                                maxima_parts(b + 1, c // (NC // 2))

                for t in range(NT):
                    if t % 4 == 1 and t > 4:
                        normalize(b, t // 4 - 1)
                        if t == 5 and not last:
                            diagonal(b + 1)
                    more(AFTER_TILE[t])
                more(AFTER_LAST[0])
                normalize(b, QUADS - 1)
                more(AFTER_LAST[1] + AFTER_LAST[2])
                residual(b)
                more(AFTER_LAST[3])
                first_stats(b)
                more(NC)
                if not last:
                    maxima_rows(b + 1)
                first_norm(b)
                second_mean(b)

            maxima_rows(0)
            body(0, first=True)
            peeled = own.n
            with dve.Fori(1, B - 1) as b:
                own.rebase(peeled + (b - 1) * LINKS)
                body(b)
                assert own.n == LINKS, own.n
            own.rebase(peeled + (B - 2) * LINKS)
            body(B - 1, last=True)
            for k in range(2):
                link(v.memset(xinT[k][D:P, :], 1.0))
                link(v.memset(w1s[k][D:P, :], 0.0))
            v.nop().then_inc(ready_v, 1)
            route(B - 1)
            slots_of(B - 1)
            second_variance(B - 1)

            def results(step, n, pair):
                before = not (isinstance(step, int) and step == 0)
                k, i0 = n // NSTEP, n % NSTEP * SI
                x = xin[k][:, i0:i0 + SI, :]
                if n % NSTEP == 0:
                    dve.wait_ge(w_in[k], W_LOADS * (pair + 1))
                    if k == 1:
                        for m in range(2):
                            need(dve, out_in[m], 16 * SI * (pair * NSTEP))
                    elif before:
                        for m in range(2):
                            dve.wait_ge(out_in[m], 16 * SI * (pair * NSTEP - NSTEP + (NSTEP + 1 - m) // 2))
                    link(v.tensor_copy(ids[k], xin[k][:, :, D]))
                dve.wait_ge(rback_mm, step + 1)
                v.tensor_tensor(res, ps[:, 7, 0:SI * D].rearrange("p (i d) -> p i d", i=SI),
                                bc(x[:, :, D + 1], D, SI), ALU.mult).then_inc(res_ok, 1)
                if before:
                    squared = own.put(v.tensor_tensor(square, cent[(n + 1) % 2], cent[(n + 1) % 2], ALU.mult))
                dve.wait_ge(res_ok, step + 1)
                marked = own.put(v.tensor_scalar(bad, res, 0.0, 0.0, ALU.mult, ALU.not_equal))
                clipped = own.put(v.tensor_scalar(subst, res, -1e4, 1e4, ALU.max, ALU.min))
                if before:
                    own.after(squared)
                    summed = own.put(v.tensor_reduce(fst[:, 4, :], square, AX, ALU.add))
                compared = own.put(v.tensor_tensor(same, res, res, ALU.is_equal))
                if before:
                    own.after(summed)
                    v.tensor_scalar(fst[:, 1, :], fst[:, 4, :], 1.0 / D, EPS, ALU.mult, ALU.add).then_inc(fvar_ok, 1)
                own.after(compared)
                link(v.tensor_tensor(subst, subst, same, ALU.mult))
                apart(dve)
                link(v.copy_predicated(res, bad, subst))
                added = own.put(v.tensor_tensor(total, res, x[:, :, 0:D], ALU.add))
                if before:
                    second_norm_of(step - 1, n - 1 if n else 2 * NSTEP - 1, pair if n else pair - 1)
                own.after(added)
                link(v.tensor_reduce(fst[:, 0, :], total, AX, ALU.add))
                link(v.tensor_scalar(fst[:, 3, :], fst[:, 0, :], 1.0 / D, None, ALU.mult))
                link(v.tensor_tensor(cent[n % 2], total, bc(fst[:, 3, :], D, SI), ALU.subtract))

            def second_norm_of(step, n, pair):
                dve.wait_ge(frstd_ok, step + 1)
                need(dve, out_in[n % 2], 16 * SI * (pair * NSTEP + n // 2))
                v.tensor_tensor(fin[n % 2], cent[n % 2], bc(fst[:, 2, :], D, SI), ALU.mult).then_inc(fin_ok, 1)

            def experts(pair):
                for n in range(2 * NSTEP):
                    results(pair * 2 * NSTEP + n, n, pair)

            base = own.base + own.n
            own.rebase(base)
            experts(0)
            peeled = own.n
            with dve.Fori(1, E // 2) as pair:
                own.rebase(base + peeled + (pair - 1) * LINKS_B)
                experts(pair)
                assert own.n == LINKS_B, own.n
            own.rebase(base + peeled + (E // 2 - 1) * LINKS_B)
            last = cent[(2 * NSTEP - 1) % 2]
            link(v.tensor_tensor(square, last, last, ALU.mult))
            link(v.tensor_reduce(fst[:, 4, :], square, AX, ALU.add))
            v.tensor_scalar(fst[:, 1, :], fst[:, 4, :], 1.0 / D, EPS, ALU.mult, ALU.add).then_inc(fvar_ok, 1)
            second_norm_of(E * NSTEP - 1, 2 * NSTEP - 1, E // 2 - 1)


_INS = ["x", "L0_tok_W", "L0_attn_w_qkv", "L0_attn_b_qkv", "L0_attn_w_proj", "L0_attn_b_proj", "L0_ffn_gate_w",
        "L0_ffn_gate_b", "L0_ffn_w1", "L0_ffn_b1", "L0_ffn_w2", "L0_ffn_b2"]


def kernel(**inputs):
    import concourse.bacc as _bacc
    from concourse.bass_utils import run_bass_kernel_spmd as _run

    nc = _bacc.Bacc("TRN2", target_bir_lowering=False, num_devices=1)
    arrays, args = {}, []
    for name in _INS:
        a = np.ascontiguousarray(inputs[name])
        arrays[f"in_{name}"] = a
        args.append(nc.dram_tensor(f"in_{name}", a.shape, mybir.dt.from_np(a.dtype), kind="ExternalInput").ap())
    arrays["in_consts"] = constants()
    args.append(nc.dram_tensor("in_consts", (P, NCONST), F32, kind="ExternalInput").ap())
    args.append(nc.dram_tensor("out_0", (B, L, D), F32, kind="ExternalOutput").ap())
    build(nc, *args)
    r = _run(nc, [arrays], core_ids=[0])
    return r.results[0]["out_0"]
```
